# Optimizing a Trainium2 kernel written in Bass

```python
import numpy as np
import jax
import jax.numpy as jnp

def _softmax(x, axis=-1):
    return jax.nn.softmax(x, axis=axis)

def _gelu(x):
    return jax.nn.gelu(x, approximate=True)

def _silu(x):
    return jax.nn.silu(x)

def _sigmoid(x):
    return jax.nn.sigmoid(x)

def _layernorm(x, axis=-1, eps=1e-05):
    m = jnp.mean(x, axis=axis, keepdims=True)
    v = jnp.var(x, axis=axis, keepdims=True)
    return (x - m) / jnp.sqrt(v + eps)

def _scatter_add(tgt, idx, src, axis=0):
    return tgt.at[idx].add(src)

def _segment_sum(src, seg, n):
    return jax.ops.segment_sum(src, seg, n)
kernel_name = 'mk_adj_preln_d1_adj_r2_1bf779'

def setup_inputs(seed: int=0):
    np.random.seed(seed)
    _w = jnp.asarray

    def _rec_inputs():
        import jax
        import jax.numpy as jnp
        _gk = jax.random.key(seed)
        x = 0.0002141 + 1 * jax.random.normal(jax.random.fold_in(_gk, 1), (128, 64, 384), jnp.float32)
        _a = jax.random.bernoulli(jax.random.fold_in(_gk, 2), 0.125, (128, 64, 64))
        _a = jnp.logical_or(_a, jnp.swapaxes(_a, -1, -2))
        _a = jnp.logical_or(_a, jnp.eye(64, dtype=bool))
        adj = _a.astype(jnp.int32)
        return (x, adj)
    x, adj = _rec_inputs()

    def _L0_gnn_setup():
        import jax, jax.numpy as jnp
        import numpy as np
        B, S, HID, DEP, DS, NTYPES = (8, 128, 384, 64, 384, 45)
        NEG = -1000000000.0
        key = jax.random.key(seed)
        ks = jax.random.split(key, 10)
        sc = lambda fan_in: 1.0 / np.sqrt(fan_in)
        return {'h': jax.random.normal(ks[0], (B, S, HID), dtype=jnp.float32), 'dep_type_matrix': jax.random.randint(ks[1], (B, S, S), 0, NTYPES), 'dep_emb_table': jax.random.normal(ks[2], (NTYPES, DEP), dtype=jnp.float32), 'W1_w': jax.random.normal(ks[3], (HID + DEP, DS), dtype=jnp.float32) * sc(HID + DEP), 'W1_b': jnp.zeros((DS,), dtype=jnp.float32), 'W2_w': jax.random.normal(ks[4], (HID + DEP, DS), dtype=jnp.float32) * sc(HID + DEP), 'W2_b': jnp.zeros((DS,), dtype=jnp.float32), 'gcn_w': jax.random.normal(ks[5], (HID, HID), dtype=jnp.float32) * sc(HID), 'gcn_b': jnp.zeros((HID,), dtype=jnp.float32), 'Wo_w': jax.random.normal(ks[6], (DS, HID), dtype=jnp.float32) * sc(DS), 'Wo_b': jnp.zeros((HID,), dtype=jnp.float32)}
    _L0_gnn_all = _L0_gnn_setup()
    _L0_gnn_in = {k: v for k, v in _L0_gnn_all.items() if k in ('dep_emb_table', 'W1_w', 'W1_b', 'W2_w', 'W2_b', 'gcn_w', 'gcn_b', 'Wo_w', 'Wo_b')}
    del _L0_gnn_all
    return {'x': x, 'adj': adj, 'L0_gnn_dep_emb_table': _L0_gnn_in['dep_emb_table'], 'L0_gnn_W1_w': _L0_gnn_in['W1_w'], 'L0_gnn_W1_b': _L0_gnn_in['W1_b'], 'L0_gnn_W2_w': _L0_gnn_in['W2_w'], 'L0_gnn_W2_b': _L0_gnn_in['W2_b'], 'L0_gnn_gcn_w': _L0_gnn_in['gcn_w'], 'L0_gnn_gcn_b': _L0_gnn_in['gcn_b'], 'L0_gnn_Wo_w': _L0_gnn_in['Wo_w'], 'L0_gnn_Wo_b': _L0_gnn_in['Wo_b']}

def reference(x, adj, L0_gnn_dep_emb_table, L0_gnn_W1_w, L0_gnn_W1_b, L0_gnn_W2_w, L0_gnn_W2_b, L0_gnn_gcn_w, L0_gnn_gcn_b, L0_gnn_Wo_w, L0_gnn_Wo_b):
    import jax
    import jax.numpy as jnp

    def _L0_gnn_ref(h, dep_type_matrix, dep_emb_table, W1_w, W1_b, W2_w, W2_b, gcn_w, gcn_b, Wo_w, Wo_b):
        import jax, jax.numpy as jnp
        import numpy as np
        B, S, HID, DEP, DS, NTYPES = (8, 128, 384, 64, 384, 45)
        NEG = -1000000000.0
        adj = dep_type_matrix != 0
        dep_emb = dep_emb_table[dep_type_matrix]
        hi_t = jnp.einsum('bid,de->bie', h, W1_w[:HID])[:, :, None, :] + jnp.einsum('bijd,de->bije', dep_emb, W1_w[HID:]) + W1_b
        hj_t = jnp.einsum('bjd,de->bje', h, W2_w[:HID])[:, None, :, :] + jnp.einsum('bijd,de->bije', dep_emb, W2_w[HID:]) + W2_b
        relevance = jnp.sum(hi_t * hj_t, axis=-1)
        masked = jnp.where(adj, relevance, NEG)
        A = jax.nn.softmax(masked, axis=2)
        h_syn = h
        for _ in range(1):
            aggregated = jnp.einsum('bij,bjd->bid', A, h_syn)
            h_syn = jax.nn.relu(aggregated @ gcn_w + gcn_b)
        return h_syn @ Wo_w + Wo_b
    h = jnp.maximum(_layernorm(x, axis=-1), 0.0)
    x = x + _L0_gnn_ref(h, adj, L0_gnn_dep_emb_table, L0_gnn_W1_w, L0_gnn_W1_b, L0_gnn_W2_w, L0_gnn_W2_b, L0_gnn_gcn_w, L0_gnn_gcn_b, L0_gnn_Wo_w, L0_gnn_Wo_b)
    return x

_drawn_inputs = setup_inputs


def setup_inputs(seed=0):
    import zlib

    import numpy as np

    out = dict(_drawn_inputs(seed))
    spreads = {'L0_gnn_W1_b': (0.0, 0.1),
     'L0_gnn_W2_b': (0.0, 0.1),
     'L0_gnn_gcn_b': (0.0, 0.1),
     'L0_gnn_Wo_b': (0.0, 0.1)}
    factors = {}
    for name, (base, spread) in spreads.items():
        noise = np.random.default_rng([zlib.crc32(name.encode()), seed]).standard_normal(out[name].shape)
        drawn = base * np.exp(spread * noise) if base else spread * noise
        out[name] = jnp.asarray(drawn.astype(out[name].dtype))
    for name, factor in factors.items():
        out[name] = (out[name] * factor).astype(out[name].dtype)
    return out
```

```python
import concourse.bass as bass
from concourse import mybir
from contextlib import ExitStack


def gnn_layer_program(nc, x, adj, emb, W1, b1, W2, b2, gcn_w, gcn_b, Wo, bo, out):
    f32, f16, i32 = mybir.dt.float32, mybir.dt.float16, mybir.dt.int32
    ALU, ACT, AX = mybir.AluOpType, mybir.ActivationFunctionType, mybir.AxisListType
    ABSMAX = bass.bass_isa.ReduceOp.absmax

    P = 128
    GRAPHS, S, D = x.shape
    NT, DE = emb.shape
    DC = D // P
    KT = 4
    GT = P // S
    N = KT * P
    NSUP = GRAPHS * S // N
    EDGE = 1
    EPS = 1e-5
    HIDDEN = -1e30

    H_SCALE = 2.0 ** 10
    W_TOP = 2.0 ** 13
    PROJ = 2.0 ** -18
    A_SCALE = 2.0 ** 14
    Z_DOWN = 2.0 ** -14
    Y_SCALE = H_SCALE * PROJ
    S_SCALE = Y_SCALE * H_SCALE
    TINY = 2.0 ** -40
    EXP_MASK = 0x7F800000
    EXP_FLIP = 254 << 23
    COEF_STEPS = 20

    W_COLS = D + 2 * NT
    x_rows = x.rearrange("(s k g) i d -> s (g i) k d", s=NSUP, k=KT, g=GT)
    out_rows = out.rearrange("(s k g) i d -> s (g i) k d", s=NSUP, k=KT, g=GT)
    adj_rows = adj.rearrange("(t g) i j -> (g i) t j", g=GT)

    ctx = ExitStack()
    with ctx:
        def sb(name, shape, dt=f32):
            return ctx.enter_context(nc.sbuf_tensor(name, shape, dt))

        def sem(name):
            return ctx.enter_context(nc.semaphore(name))

        w1_dep = sb("w1_dep", [DE, D])
        w2_dep = sb("w2_dep", [DE, D])
        emb_raw = sb("emb_raw", [NT, DE])
        embT = sb("embT", [DE, NT])
        b1_col = sb("b1_col", [P, DC])
        b2_col = sb("b2_col", [P, DC])
        pT = sb("pT", [P, DC, NT])
        qT = sb("qT", [P, DC, NT])
        pqT = sb("pqT", [P, DC, NT])
        pq_row = sb("pq_row", [P, NT])
        gcn_raw = sb("gcn_raw", [P, DC, D + 1])
        wo_raw = sb("wo_raw", [P, DC, D])
        bo_all = sb("bo_all", [P, 1, D])
        ident = sb("ident", [P, P])
        ones = sb("ones", [P, P])
        peak_part = sb("peak_part", [P, 3])
        peak = sb("peak", [P, 3])
        peak_bits = sb("peak_bits", [P, 3], i32)
        flip_bits = sb("flip_bits", [P, 3], i32)
        unscale = sb("unscale", [P, 3])
        scale = sb("scale", [P, 3])
        exp_scale = sb("exp_scale", [P, 1])
        exp_nscale = sb("exp_nscale", [P, 1])
        out_scale = sb("out_scale", [P, 1])
        out_half = sb("out_half", [P, 1])
        pair_bias = sb("pair_bias", [P, DC])
        pq_scaled = sb("pq_scaled", [P, 1])
        gcn_bias = sb("gcn_bias", [P, DC])
        m_hi = sb("m_hi", [P, DC, D], f16)
        m_lo = sb("m_lo", [P, DC, D], f16)
        gw_hi = sb("gw_hi", [P, DC, D + 1], f16)
        gw_lo = sb("gw_lo", [P, DC, D + 1], f16)
        wo_hi = sb("wo_hi", [P, DC, D], f16)
        wo_lo = sb("wo_lo", [P, DC, D], f16)

        x_all = sb("x_all", [P, NSUP, KT, D])
        adj_all = sb("adj_all", [P, NSUP * KT, S], i32)[:, :, :]
        bias_all = adj_all.bitcast(f32)
        w1_raw, w2_raw, w1T, w2T = (x_all[:, NSUP - 4 + n, 0:DC, :] for n in range(4))
        m32, gw32, wo32 = w1_raw, gcn_raw, wo_raw
        stats6 = sb("stats6", [P, KT, 6])
        var_d = sb("var_d", [P, KT])[:, :]
        root = sb("root", [P, KT])[:, :]
        root_sq = sb("root_sq", [P, KT])[:, :]
        const_values = {"spread": D / 4, "d_eps": D * EPS, "minus_half": -0.5, "three_halves": 1.5,
                        "h_scale": H_SCALE * D ** 0.5}
        const_all = sb("const_all", [P, len(const_values), KT])
        const = {name: const_all[:, n, :] for n, name in enumerate(const_values)}
        ln_mul = sb("ln_mul", [P, KT])[:, :]
        ln_add = sb("ln_add", [P, KT])[:, :]
        h_tok = sb("h_tok", [P, KT, D])
        hT_hi = sb("hT_hi", [P, DC, N], f16)
        hT_lo = sb("hT_lo", [P, DC, N], f16)
        g32 = sb("g32", [P, DC, N])
        pair = g32[:, :, 0:W_COLS]
        g_hi = sb("g_hi", [P, DC, N], f16)
        g_lo = sb("g_lo", [P, DC, N], f16)
        hg_hi = sb("hg_hi", [P, KT, D], f16)
        hg_lo = sb("hg_lo", [P, KT, D], f16)
        row_term = sb("row_term", [P, KT])
        edge_bias = sb("edge_bias", [P, KT, P])
        scores = sb("scores", [P, KT, P])
        row_max = sb("row_max", [P, KT])
        exp_bias = sb("exp_bias", [P, KT])
        row_sum = sb("row_sum", [P, KT])
        row_inv = sb("row_inv", [P, KT])
        att = sb("att", [P, KT, P])
        attT_hi = sb("attT_hi", [P, N], f16)
        attT_lo = sb("attT_lo", [P, N], f16)
        z32 = sb("z32", [P, DC, N])
        z_hi = sb("z_hi", [P, DC, N], f16)
        z_lo = sb("z_lo", [P, DC, N], f16)

        bank = [ctx.enter_context(nc.psum_tensor(f"bank{i}", [P, 512], f32)) for i in range(8)]
        G_BANK, Z_BANK, HG_BANK, T_BANK, O_BANK = (0, 1, 2), (3, 4, 5), (0, 1, 2, 3), (4, 5, 0), (1, 2, 3, 4)
        score_bank, attT_bank = bank[6], bank[7]

        names = """w12_loaded dep_loaded gcn_loaded wo_loaded bo_loaded adj_loaded adj0_loaded x_loaded
            ident_zeroed ident_made ones_made cross_hidden w_transposed w_copied emb_transposed emb_copied
            pq_projected pq_biased pq_multiplied pairs_done pairs_copied part_peaks peaks_reduced
            scale_step scales_ready m_scaled m_high m_split gw_scaled gw_high gw_split wo_scaled wo_high wo_split
            consts_made bias_made stats_ready coef_ready h_ready
            t_done t_high t_split g_done g_copied g_high g_split hg_done hg_high hg_split
            s_done edge_ready scored maxed exp_bias_ready exp_done inverted att_ready
            attT_done attT_high attT_split z_done z_copied z_high z_split o_done o_added x_biased stored""".split()
        sems = {n: sem(n) for n in names}
        (w12_loaded, dep_loaded, gcn_loaded, wo_loaded, bo_loaded, adj_loaded, adj0_loaded, x_loaded,
         ident_zeroed, ident_made, ones_made, cross_hidden, w_transposed, w_copied, emb_transposed, emb_copied,
         pq_projected, pq_biased, pq_multiplied, pairs_done, pairs_copied, part_peaks, peaks_reduced,
         scale_step, scales_ready, m_scaled, m_high, m_split, gw_scaled, gw_high, gw_split, wo_scaled, wo_high,
         wo_split, consts_made, bias_made, stats_ready, coef_ready, h_ready,
         t_done, t_high, t_split, g_done, g_copied, g_high, g_split, hg_done, hg_high, hg_split,
         s_done, edge_ready, scored, maxed, exp_bias_ready, exp_done, inverted, att_ready,
         attT_done, attT_high, attT_split, z_done, z_copied, z_high, z_split, o_done, o_added, x_biased,
         stored) = [sems[n] for n in names]

        block = ctx.enter_context(nc.Block())
        LAST = NSUP - 1

        @block.sync
        def _(sp):
            def load_x(s):
                sp.dma_start(x_all[:, s, :, :], x_rows[s, :, :, :]).then_inc(x_loaded, 16)

            def store_out(s):
                sp.wait_ge(o_added, KT * (s + 1))
                sp.dma_start(out_rows[s, :, :, :], x_all[:, s, :, :]).then_inc(stored, 16)

            load_x(0)
            for s in range(1, 4):
                sp.wait_ge(x_loaded, 16 * s)
                load_x(s)
            with sp.Fori(0, NSUP - 4) as s:
                sp.wait_ge(x_loaded, 16 * (s + 4))
                load_x(s + 4)
                store_out(s)
            with sp.Fori(NSUP - 4, NSUP) as s:
                store_out(s)
            sp.wait_ge(stored, 16 * NSUP)

        @block.gpsimd
        def _(pool):
            nc.gpsimd.memset(ident[:, :], 0.0).then_inc(ident_zeroed, 1)
            nc.gpsimd.memset(ones[:, :], 1.0).then_inc(ones_made, 1)
            nc.gpsimd.memset(edge_bias[:, :, :], 2 * HIDDEN).then_inc(cross_hidden, 1)
            pool.wait_ge(ident_zeroed, 1)
            nc.gpsimd.affine_select(out=ident[:, :], in_=ident[:, :], compare_op=ALU.not_equal, fill=1.0,
                                    base=0, pattern=[[-1, P]], channel_multiplier=1).then_inc(ident_made, 1)

            def coefficients(s):
                mean_e, mean_o, m2_e, m2_o = (stats6[:, :, n] for n in (1, 4, 2, 5))
                steps = [(root_sq, mean_e, mean_o, ALU.subtract),
                         (root_sq, root_sq, root_sq, ALU.mult),
                         (root_sq, root_sq, const["spread"], ALU.mult),
                         (var_d, m2_e, m2_o, ALU.add),
                         (var_d, var_d, root_sq, ALU.add),
                         (var_d, var_d, const["d_eps"], ALU.add),
                         (root, var_d, const["minus_half"], ALU.pow),
                         (var_d, var_d, const["minus_half"], ALU.mult)]
                steps += [(root_sq, root, root, ALU.mult), (root_sq, root_sq, var_d, ALU.mult),
                          (root_sq, root_sq, const["three_halves"], ALU.add), (root, root, root_sq, ALU.mult)] * 2
                steps += [(ln_mul, root, const["h_scale"], ALU.mult),
                          (root_sq, mean_e, mean_o, ALU.add),
                          (root_sq, root_sq, ln_mul, ALU.mult),
                          (ln_add, root_sq, const["minus_half"], ALU.mult)]
                assert len(steps) == COEF_STEPS
                pool.wait_ge(stats_ready, s + 1)
                if not isinstance(s, int) or s >= 1:
                    pool.wait_ge(h_ready, s)
                for n, (dst, in0, in1, op) in enumerate(steps):
                    if n:
                        pool.wait_ge(coef_ready, COEF_STEPS * s + n)
                    nc.gpsimd.tensor_tensor(dst, in0, in1, op).then_inc(coef_ready, 1)

            def edge_masks(s):
                for g in range(GT):
                    rows = slice(g * S, (g + 1) * S)
                    bias = bias_all[rows, bass.ds(KT * s, KT), :]
                    nc.gpsimd.tensor_tensor(edge_bias[rows, :, g * S:(g + 1) * S], bias,
                                            ones[rows, 0:S].unsqueeze(1).broadcast_to([S, KT, S]),
                                            ALU.mult).then_inc(edge_ready, 1)
                pool.wait_ge(edge_ready, GT * (s + 1))

            for n, value in enumerate(const_values.values()):
                ins = nc.gpsimd.memset(const_all[:, n, :], value)
            ins.then_inc(consts_made, 1)
            pool.wait_ge(consts_made, 1)
            pool.wait_ge(ones_made, 1)
            coefficients(0)
            coefficients(1)
            pool.wait_ge(cross_hidden, 1)
            pool.wait_ge(adj0_loaded, 16)
            nc.gpsimd.tensor_scalar(bias_all[:, 0:KT, :], adj_all[:, 0:KT, :], -1.0, -HIDDEN,
                                    ALU.add, ALU.mult).then_inc(bias_made, 1)
            pool.wait_ge(bias_made, 1)
            edge_masks(0)
            pool.wait_ge(bo_loaded, 16)
            pool.wait_ge(part_peaks, 3)
            nc.gpsimd.partition_all_reduce(peak[:, :], peak_part[:, :], P, ABSMAX).then_inc(peaks_reduced, 1)
            pool.wait_ge(adj_loaded, 16)
            nc.gpsimd.tensor_scalar(bias_all[:, KT:, :], adj_all[:, KT:, :], -1.0, -HIDDEN,
                                    ALU.add, ALU.mult).then_inc(bias_made, 1)
            pool.wait_ge(bias_made, 2)

            def iteration(s, prev=True, cur=True, nxt=True, nxt2=True):
                if cur:
                    for c in range(DC):
                        pool.wait_ge(g_high, DC * s + c + 1)
                        nc.gpsimd.tensor_tensor(g_lo[:, c, :], g32[:, c, :], g_hi[:, c, :],
                                                ALU.subtract).then_inc(g_split, 1)
                if prev:
                    for c in range(DC):
                        pool.wait_ge(z_high, DC * (s - 1) + c + 1)
                        nc.gpsimd.tensor_tensor(z_lo[:, c, :], z32[:, c, :], z_hi[:, c, :],
                                                ALU.subtract).then_inc(z_split, 1)
                if nxt2:
                    coefficients(s + 2)
                if cur:
                    pool.wait_ge(h_ready, s + 1)
                    nc.gpsimd.tensor_tensor(x_all[:, s, :, :], x_all[:, s, :, :],
                                            bo_all[:, :, :].broadcast_to([P, KT, D]),
                                            ALU.add).then_inc(x_biased, 1)
                if nxt:
                    pool.wait_ge(scored, KT * (s + 1))
                    pool.wait_ge(x_biased, s + 1)
                    edge_masks(s + 1)

            iteration(0, prev=False)
            iteration(1)
            with pool.Fori(2, LAST - 1) as s:
                iteration(s)
            iteration(LAST - 1, nxt2=False)
            iteration(LAST, nxt=False, nxt2=False)
            iteration(LAST + 1, cur=False, nxt=False, nxt2=False)

        @block.scalar
        def _(act):
            act.dma_start(w1_raw[:, :, :], W1[0:D, :].rearrange("(c p) e -> p c e", p=P)).then_inc(w12_loaded, 16)
            act.dma_start(w2_raw[:, :, :], W2[0:D, :].rearrange("(c p) e -> p c e", p=P)).then_inc(w12_loaded, 16)
            act.dma_start(emb_raw[:, :], emb).then_inc(dep_loaded, 16)
            act.dma_start(w1_dep[:, :], W1[D:D + DE, :]).then_inc(dep_loaded, 16)
            act.dma_start(w2_dep[:, :], W2[D:D + DE, :]).then_inc(dep_loaded, 16)
            act.dma_start(b1_col[:, :], b1.rearrange("(c p) -> p c", p=P),
                          allow_slow_non_contiguous=True).then_inc(dep_loaded, 16)
            act.dma_start(b2_col[:, :], b2.rearrange("(c p) -> p c", p=P),
                          allow_slow_non_contiguous=True).then_inc(dep_loaded, 16)
            act.dma_start(gcn_raw[:, :, 0:D], gcn_w.rearrange("(c p) e -> p c e", p=P)).then_inc(gcn_loaded, 16)
            act.dma_start(gcn_raw[:, :, D:D + 1], gcn_b.rearrange("(c p o) -> p c o", p=P, o=1),
                          allow_slow_non_contiguous=True).then_inc(gcn_loaded, 16)
            act.dma_start(wo_raw[:, :, :], Wo.rearrange("(c p) e -> p c e", p=P)).then_inc(wo_loaded, 16)
            act.dma_start(adj_all[:, 0:KT, :], adj_rows[:, 0:KT, :]).then_inc(adj0_loaded, 16)
            act.dma_start(bo_all[:, 0, :], bo.partition_broadcast(P)).then_inc(bo_loaded, 16)
            act.dma_start(adj_all[:, KT:, :], adj_rows[:, KT:, :]).then_inc(adj_loaded, 16)

            def normalise(s):
                act.wait_ge(coef_ready, COEF_STEPS * (s + 1))
                if not isinstance(s, int) or s >= 1:
                    act.wait_ge(t_done, DC * s)
                for k in range(KT):
                    ins = nc.scalar.activation(h_tok[:, k, :], x_all[:, s, k, :], ACT.Relu,
                                               bias=ln_add[:, k:k + 1], scale=ln_mul[:, k:k + 1])
                ins.then_inc(h_ready, 1)

            def transposed_high(s):
                if not isinstance(s, int) or s >= 1:
                    act.wait_ge(s_done, s)
                for c in range(DC):
                    act.wait_ge(t_done, DC * s + c + 1)
                    nc.scalar.activation(hT_hi[:, c, :], bank[T_BANK[c]][:, :], ACT.Copy).then_inc(t_high, 1)

            for c in range(DC):
                act.wait_ge(w_transposed, c + 1)
                nc.scalar.activation(w1T[:, c, :], bank[c][:, 0:D], ACT.Copy).then_inc(w_copied, 1)
            normalise(0)
            for c in range(DC):
                act.wait_ge(pairs_done, c + 1)
                nc.scalar.activation(pair[:, c, 0:D], bank[c][:, 0:D], ACT.Copy).then_inc(pairs_copied, 1)
            transposed_high(0)
            normalise(1)
            act.wait_ge(scales_ready, 1)
            for c in range(DC):
                ins = nc.scalar.activation(m32[:, c, :], pair[:, c, 0:D], ACT.Copy, scale=scale[:, 0:1])
            ins.then_inc(m_scaled, 1)
            for c in range(DC):
                nc.scalar.activation(gw32[:, c, 0:D], gcn_raw[:, c, 0:D], ACT.Copy, scale=scale[:, 1:2])
                ins = nc.scalar.activation(gw32[:, c, D:D + 1], pair[:, c, D + NT + EDGE:D + NT + EDGE + 1],
                                           ACT.Copy, scale=scale[:, 0:1])
            ins.then_inc(gw_scaled, 1)
            for c in range(DC):
                ins = nc.scalar.activation(wo32[:, c, :], wo_raw[:, c, :], ACT.Copy, scale=scale[:, 2:3])
            ins.then_inc(wo_scaled, 1)

            def iteration(s, prev=True, prev2=True, cur=True, nxt=True, nxt2=True):
                for c in range(DC):
                    if cur:
                        act.wait_ge(g_done, DC * s + c + 1)
                        if prev:
                            act.wait_ge(g_split, DC * (s - 1) + c + 1)
                        nc.scalar.activation(g32[:, c, :], bank[G_BANK[c]][:, :], ACT.Identity,
                                             bias=pair_bias[:, c:c + 1], scale=PROJ).then_inc(g_copied, 1)
                    if c == 0 and prev:
                        act.wait_ge(attT_done, s)
                        if prev2:
                            act.wait_ge(z_done, DC * (s - 1))
                        nc.scalar.activation(attT_hi[:, :], attT_bank[:, :], ACT.Copy,
                                             scale=A_SCALE).then_inc(attT_high, 1)
                if prev:
                    for c in range(DC):
                        act.wait_ge(z_done, DC * (s - 1) + c + 1)
                        if prev2:
                            act.wait_ge(z_split, DC * (s - 2) + c + 1)
                        nc.scalar.activation(z32[:, c, :], bank[Z_BANK[c]][:, :], ACT.Relu,
                                             bias=gcn_bias[:, c:c + 1], scale=Z_DOWN).then_inc(z_copied, 1)
                if cur:
                    if prev:
                        act.wait_ge(z_done, DC * s)
                    for k in range(KT):
                        act.wait_ge(hg_done, KT * s + k + 1)
                        nc.scalar.activation(hg_hi[:, k, :], bank[HG_BANK[k]][:, 0:D], ACT.Copy,
                                             scale=PROJ).then_inc(hg_high, 1)
                if nxt:
                    transposed_high(s + 1)
                if cur:
                    act.wait_ge(exp_bias_ready, s + 1)
                    if prev:
                        act.wait_ge(att_ready, s)
                    for k in range(KT):
                        nc.scalar.activation(scores[:, k, :], scores[:, k, :], ACT.Exp,
                                             bias=exp_bias[:, k:k + 1], scale=exp_scale[:, 0:1],
                                             accum_out=row_sum[:, k:k + 1]).then_inc(exp_done, 1)
                if nxt2:
                    normalise(s + 2)

            act.wait_ge(gw_scaled, 1)
            iteration(0, prev=False, prev2=False)
            iteration(1, prev2=False)
            with act.Fori(2, LAST - 1) as s:
                iteration(s)
            iteration(LAST - 1, nxt2=False)
            iteration(LAST, nxt=False, nxt2=False)
            iteration(LAST + 1, cur=False, nxt=False, nxt2=False)

        @block.vector
        def _(dve):
            def statistics(s):
                dve.wait_ge(x_loaded, 16 * (s + 1))
                if not isinstance(s, int) or s >= 1:
                    dve.wait_ge(coef_ready, COEF_STEPS * s)
                for k in range(KT):
                    ins = nc.vector.bn_stats(stats6[:, k, :], x_all[:, s, k, :])
                ins.then_inc(stats_ready, 1)

            def transposed_low(s):
                for c in range(DC):
                    dve.wait_ge(t_high, DC * s + c + 1)
                    nc.vector.tensor_tensor(hT_lo[:, c, :], bank[T_BANK[c]][:, :], hT_hi[:, c, :],
                                            ALU.subtract).then_inc(t_split, 1)

            statistics(0)
            for c in range(DC):
                dve.wait_ge(w_transposed, DC + c + 1)
                nc.vector.tensor_copy(w2T[:, c, :], bank[3 + c][:, 0:D]).then_inc(w_copied, 1)
            dve.wait_ge(emb_transposed, 1)
            nc.vector.tensor_copy(embT[:, :], bank[6][0:DE, 0:NT]).then_inc(emb_copied, 1)
            dve.wait_ge(gcn_loaded, 32)
            nc.vector.tensor_reduce(peak_part[:, 1:2], gcn_raw[:, :, :], AX.XY, ALU.max,
                                    apply_absolute_value=True).then_inc(part_peaks, 1)
            dve.wait_ge(wo_loaded, 16)
            nc.vector.tensor_reduce(peak_part[:, 2:3], wo_raw[:, :, :], AX.XY, ALU.max,
                                    apply_absolute_value=True).then_inc(part_peaks, 1)
            dve.wait_ge(pq_projected, 1)
            for c in range(DC):
                nc.vector.tensor_scalar(pT[:, c, :], bank[7][:, c * NT:(c + 1) * NT], b1_col[:, c:c + 1], None,
                                        ALU.add)
                ins = nc.vector.tensor_scalar(qT[:, c, :], bank[7][:, (DC + c) * NT:(DC + c + 1) * NT],
                                              b2_col[:, c:c + 1], None, ALU.add)
            ins.then_inc(pq_biased, 1)
            dve.wait_ge(pq_biased, 1)
            nc.vector.tensor_tensor(pqT[:, :, :], pT[:, :, :], qT[:, :, :], ALU.mult).then_inc(pq_multiplied, 1)
            statistics(1)
            dve.wait_ge(pairs_done, DC + 1)
            nc.vector.tensor_copy(pair[:, :, D:W_COLS],
                                  bank[3][:, 0:2 * DC * NT].rearrange("p (c n) -> p c n", c=DC))\
              .then_inc(pairs_copied, 1)
            nc.vector.tensor_copy(pq_row[:, :], bank[4][:, 0:NT]).then_inc(pairs_copied, 1)
            dve.wait_ge(pairs_copied, DC + 2)
            nc.vector.tensor_reduce(peak_part[:, 0:1], pair[:, :, :], AX.XY, ALU.max,
                                    apply_absolute_value=True).then_inc(part_peaks, 1)
            transposed_low(0)
            dve.wait_ge(peaks_reduced, 1)
            nc.vector.tensor_scalar(peak[:, :], peak[:, :], TINY, None, ALU.max).then_inc(scale_step, 1)
            dve.wait_ge(scale_step, 1)
            nc.vector.tensor_scalar(peak_bits[:, :], peak[:, :].bitcast(i32), EXP_MASK, None,
                                    ALU.bitwise_and).then_inc(scale_step, 1)
            dve.wait_ge(scale_step, 2)
            nc.vector.tensor_scalar(flip_bits[:, :], peak_bits[:, :], -1.0, float(EXP_FLIP),
                                    ALU.mult, ALU.add).then_inc(scale_step, 1)
            nc.vector.tensor_scalar(unscale[:, :], peak_bits[:, :].bitcast(f32), 1.0 / W_TOP, None,
                                    ALU.mult).then_inc(scale_step, 1)
            dve.wait_ge(scale_step, 4)
            nc.vector.tensor_scalar(scale[:, :], flip_bits[:, :].bitcast(f32), W_TOP, None,
                                    ALU.mult).then_inc(scale_step, 1)
            nc.vector.tensor_scalar(exp_scale[:, :], unscale[:, 0:1], 1.0 / S_SCALE, None, ALU.mult)
            nc.vector.tensor_scalar(exp_nscale[:, :], unscale[:, 0:1], -1.0 / S_SCALE, None, ALU.mult)
            nc.vector.tensor_scalar(out_half[:, :], unscale[:, 1:2], 1.0 / Y_SCALE, None,
                                    ALU.mult).then_inc(scale_step, 1)
            dve.wait_ge(scale_step, 6)
            nc.vector.tensor_scalar(out_scale[:, :], out_half[:, :], unscale[:, 2:3], None, ALU.mult)
            nc.vector.tensor_scalar(pair_bias[:, :], pair[:, :, D + EDGE], scale[:, 0:1], Y_SCALE,
                                    ALU.mult, ALU.mult)
            nc.vector.tensor_scalar(pq_scaled[:, :], pq_row[:, EDGE:EDGE + 1], scale[:, 0:1], S_SCALE,
                                    ALU.mult, ALU.mult)
            nc.vector.tensor_scalar(gcn_bias[:, :], gcn_raw[:, :, D], scale[:, 1:2], Y_SCALE,
                                    ALU.mult, ALU.mult).then_inc(scales_ready, 1)
            dve.wait_ge(scales_ready, 1)
            for scaled, w32, whi, high, wlo, split in (
                    (m_scaled, m32, m_hi, m_high, m_lo, m_split), (gw_scaled, gw32, gw_hi, gw_high, gw_lo, gw_split),
                    (wo_scaled, wo32, wo_hi, wo_high, wo_lo, wo_split)):
                dve.wait_ge(scaled, 1)
                nc.vector.tensor_copy(whi[:, :, :], w32[:, :, :]).then_inc(high, 1)
                dve.wait_ge(high, 1)
                nc.vector.tensor_tensor(wlo[:, :, :], w32[:, :, :], whi[:, :, :], ALU.subtract).then_inc(split, 1)

            def iteration(s, prev=True, prev2=True, cur=True, nxt=True, nxt2=True):
                for c in range(DC):
                    if cur:
                        dve.wait_ge(g_copied, DC * s + c + 1)
                        if prev and c == 0:
                            dve.wait_ge(s_done, s)
                        nc.vector.tensor_copy(g_hi[:, c, :], g32[:, c, :]).then_inc(g_high, 1)
                    if c == 0 and prev:
                        dve.wait_ge(attT_high, s)
                        nc.vector.scalar_tensor_tensor(attT_lo[:, :], attT_bank[:, :], A_SCALE, attT_hi[:, :],
                                                       ALU.mult, ALU.subtract).then_inc(attT_split, 1)
                if prev:
                    for c in range(DC):
                        dve.wait_ge(z_copied, DC * (s - 1) + c + 1)
                        if prev2 and c == 0:
                            dve.wait_ge(o_done, KT * (s - 1))
                        nc.vector.tensor_copy(z_hi[:, c, :], z32[:, c, :]).then_inc(z_high, 1)
                if cur:
                    for k in range(KT):
                        dve.wait_ge(hg_high, KT * s + k + 1)
                        nc.vector.tensor_scalar(row_term[:, k:k + 1], bank[HG_BANK[k]][:, D:D + 1], Y_SCALE,
                                                pq_scaled[:, 0:1], ALU.mult, ALU.add)
                        nc.vector.scalar_tensor_tensor(hg_lo[:, k, :], bank[HG_BANK[k]][:, 0:D], PROJ,
                                                       hg_hi[:, k, :], ALU.mult, ALU.subtract)\
                          .then_inc(hg_split, 1)
                    dve.wait_ge(s_done, s + 1)
                    dve.wait_ge(edge_ready, GT * (s + 1))
                    dve.wait_ge(hg_split, KT * (s + 1))
                    for k in range(KT):
                        nc.vector.scalar_tensor_tensor(scores[:, k, :], score_bank[:, k * P:(k + 1) * P],
                                                       row_term[:, k:k + 1], edge_bias[:, k, :],
                                                       ALU.add, ALU.add).then_inc(scored, 1)
                    dve.wait_ge(scored, KT * (s + 1))
                    nc.vector.tensor_reduce(row_max[:, :], scores[:, :, :], AX.X, ALU.max).then_inc(maxed, 1)
                    dve.wait_ge(maxed, s + 1)
                    nc.vector.tensor_scalar(exp_bias[:, :], row_max[:, :], exp_nscale[:, 0:1], None,
                                            ALU.mult).then_inc(exp_bias_ready, 1)
                if nxt:
                    transposed_low(s + 1)
                if nxt2:
                    statistics(s + 2)
                if cur:
                    dve.wait_ge(exp_done, KT * (s + 1))
                    nc.vector.reciprocal(row_inv[:, :], row_sum[:, :]).then_inc(inverted, 1)
                    dve.wait_ge(inverted, s + 1)
                    if prev:
                        dve.wait_ge(attT_done, s)
                    nc.vector.tensor_tensor(att[:, :, :], scores[:, :, :],
                                            row_inv[:, :].unsqueeze(2).broadcast_to([P, KT, P]),
                                            ALU.mult).then_inc(att_ready, 1)
                if prev:
                    dve.wait_ge(x_biased, s)
                    for k in range(KT):
                        dve.wait_ge(o_done, KT * (s - 1) + k + 1)
                        nc.vector.scalar_tensor_tensor(x_all[:, s - 1, k, :], bank[O_BANK[k]][:, 0:D],
                                                       out_scale[:, 0:1], x_all[:, s - 1, k, :],
                                                       ALU.mult, ALU.add).then_inc(o_added, 1)

            iteration(0, prev=False, prev2=False)
            iteration(1, prev2=False)
            with dve.Fori(2, LAST - 1) as s:
                iteration(s)
            iteration(LAST - 1, nxt2=False)
            iteration(LAST, nxt=False, nxt2=False)
            iteration(LAST + 1, cur=False, nxt=False, nxt2=False)

        @block.tensor
        def _(pe):
            def split_product(dst, left, right, chunks=DC):
                last = None
                for c in range(chunks):
                    (lh, ll), (rh, rl) = left(c), right(c)
                    nc.tensor.matmul(dst, lh, rh, start=(c == 0), stop=False)
                    nc.tensor.matmul(dst, lh, rl, start=False, stop=False)
                    last = nc.tensor.matmul(dst, ll, rh, start=False, stop=(c == chunks - 1))
                return last

            pe.wait_ge(w12_loaded, 32)
            pe.wait_ge(ident_made, 1)
            for n, raw in ((0, w1_raw), (DC, w2_raw)):
                for c in range(DC):
                    for d in range(DC):
                        last = nc.tensor.transpose(bank[n + c][:, d * P:(d + 1) * P],
                                                   raw[:, d, c * P:(c + 1) * P], ident[:, :])
                    last.then_inc(w_transposed, 1)
            pe.wait_ge(dep_loaded, 16 * 5)
            nc.tensor.transpose(bank[6][0:DE, 0:NT], emb_raw[:, :], ident[0:NT, 0:NT]).then_inc(emb_transposed, 1)
            pe.wait_ge(emb_copied, 1)
            for n, dep in ((0, w1_dep), (DC, w2_dep)):
                for c in range(DC):
                    last = nc.tensor.matmul(bank[7][:, (n + c) * NT:(n + c + 1) * NT], dep[:, c * P:(c + 1) * P],
                                            embT[:, :], start=True, stop=True)
            last.then_inc(pq_projected, 1)
            pe.wait_ge(w_copied, 2 * DC)
            for d in range(DC):
                for c in range(DC):
                    last = nc.tensor.matmul(bank[d][:, 0:D], w1T[:, c, d * P:(d + 1) * P], w2T[:, c, :],
                                            start=(c == 0), stop=(c == DC - 1))
                last.then_inc(pairs_done, 1)
            pe.wait_ge(pq_multiplied, 1)
            for d in range(DC):
                for n, (wT, vT) in enumerate(((w2T, pT), (w1T, qT))):
                    at = (2 * d + n) * NT
                    for c in range(DC):
                        nc.tensor.matmul(bank[3][:, at:at + NT], wT[:, c, d * P:(d + 1) * P], vT[:, c, :],
                                         start=(c == 0), stop=(c == DC - 1))
            pe.wait_ge(ones_made, 1)
            for c in range(DC):
                last = nc.tensor.matmul(bank[4][:, 0:NT], ones[:, :], pqT[:, c, :],
                                        start=(c == 0), stop=(c == DC - 1))
            last.then_inc(pairs_done, 1)

            def transposes(s, prev=True):
                pe.wait_ge(h_ready, s + 1)
                for c in range(DC):
                    if prev and c < 2:
                        pe.wait_ge(z_copied, DC * (s - 2) + c + 2)
                    if c == 2 and (not isinstance(s, int) or s >= 1):
                        pe.wait_ge(hg_split, KT * (s - 1) + 1)
                    for k in range(KT):
                        last = nc.tensor.transpose(bank[T_BANK[c]][:, k * P:(k + 1) * P],
                                                   h_tok[:, k, c * P:(c + 1) * P], ident[:, :])
                    last.then_inc(t_done, 1)

            pe.wait_ge(pairs_copied, DC + 2)
            transposes(0, prev=False)
            pe.wait_ge(m_split, 1)

            def iteration(s, prev=True, prev2=True, cur=True, nxt=True, nxt2=True):
                for c in range(DC):
                    if cur:
                        if c == 0:
                            pe.wait_ge(t_split, DC * (s + 1))
                        elif prev2:
                            pe.wait_ge(o_added, KT * (s - 2) + c)
                        split_product(bank[G_BANK[c]][:, :],
                                      lambda d: (m_hi[:, d, c * P:(c + 1) * P], m_lo[:, d, c * P:(c + 1) * P]),
                                      lambda d: (hT_hi[:, d, :], hT_lo[:, d, :])).then_inc(g_done, 1)
                    if c == 0 and prev:
                        pe.wait_ge(att_ready, s)
                        if prev2:
                            pe.wait_ge(attT_split, s - 1)
                        for k in range(KT):
                            last = nc.tensor.transpose(attT_bank[:, k * P:(k + 1) * P], att[:, k, :], ident[:, :])
                        last.then_inc(attT_done, 1)
                if prev:
                    pe.wait_ge(attT_split, s)
                    pe.wait_ge(hg_split, KT * s)
                    for c in range(DC):
                        if prev2 and c < 2:
                            pe.wait_ge(o_added, KT * (s - 2) + c + 3)
                        for k in range(KT):
                            rows = slice(k * P, (k + 1) * P)
                            last = split_product(
                                bank[Z_BANK[c]][:, rows],
                                lambda _: (hg_hi[:, k, c * P:(c + 1) * P], hg_lo[:, k, c * P:(c + 1) * P]),
                                lambda _: (attT_hi[:, rows], attT_lo[:, rows]), chunks=1)
                        last.then_inc(z_done, 1)
                if cur:
                    if not prev:
                        pe.wait_ge(gw_split, 1)
                    for k in range(KT):
                        rows = slice(k * P, (k + 1) * P)
                        if k < DC:
                            pe.wait_ge(g_copied, DC * s + k + 1)
                        elif prev:
                            pe.wait_ge(z_copied, DC * (s - 1) + 1)
                        split_product(bank[HG_BANK[k]][:, 0:D + 1],
                                      lambda d: (hT_hi[:, d, rows], hT_lo[:, d, rows]),
                                      lambda d: (gw_hi[:, d, :], gw_lo[:, d, :])).then_inc(hg_done, 1)
                    pe.wait_ge(g_split, DC * (s + 1))
                    if prev:
                        pe.wait_ge(scored, KT * s)
                    for k in range(KT):
                        rows = slice(k * P, (k + 1) * P)
                        last = split_product(score_bank[:, rows],
                                             lambda d: (g_hi[:, d, rows], g_lo[:, d, rows]),
                                             lambda d: (hT_hi[:, d, rows], hT_lo[:, d, rows]))
                    last.then_inc(s_done, 1)
                if nxt:
                    transposes(s + 1, prev=prev)
                if prev:
                    pe.wait_ge(z_split, DC * s)
                    for k in range(KT):
                        rows = slice(k * P, (k + 1) * P)
                        if not cur:
                            pe.wait_ge(o_added, KT * (s - 2) + k + 1)
                        elif k < DC:
                            pe.wait_ge(hg_split, KT * s + k + 2)
                        elif nxt:
                            pe.wait_ge(t_split, DC * (s + 1) + 1)
                        split_product(bank[O_BANK[k]][:, 0:D],
                                      lambda e: (z_hi[:, e, rows], z_lo[:, e, rows]),
                                      lambda e: (wo_hi[:, e, :], wo_lo[:, e, :])).then_inc(o_done, 1)

            iteration(0, prev=False, prev2=False)
            pe.wait_ge(wo_split, 1)
            iteration(1, prev2=False)
            with pe.Fori(2, LAST - 1) as s:
                iteration(s)
            iteration(LAST - 1, nxt2=False)
            iteration(LAST, nxt=False, nxt2=False)
            iteration(LAST + 1, cur=False, nxt=False, nxt2=False)


_INS = ['x', 'adj', 'L0_gnn_dep_emb_table', 'L0_gnn_W1_w', 'L0_gnn_W1_b', 'L0_gnn_W2_w', 'L0_gnn_W2_b',
        'L0_gnn_gcn_w', 'L0_gnn_gcn_b', 'L0_gnn_Wo_w', 'L0_gnn_Wo_b']


def kernel(**inputs):
    import numpy as _np
    import concourse.bacc as _bacc
    from concourse import mybir as _mybir
    from concourse.bass_utils import run_bass_kernel_spmd as _run

    nc = _bacc.Bacc("TRN2", target_bir_lowering=False, num_devices=1)
    arrays, args = {}, []
    for name in _INS:
        a = _np.ascontiguousarray(inputs[name])
        arrays[f"in_{name}_dram"] = a
        args.append(nc.dram_tensor(f"in_{name}_dram", a.shape, _mybir.dt.from_np(a.dtype), kind="ExternalInput").ap())
    shape = inputs['x'].shape
    args.append(nc.dram_tensor("out_0_dram", shape, _mybir.dt.float32, kind="ExternalOutput").ap())
    gnn_layer_program(nc, *args)
    r = _run(nc, [arrays], core_ids=[0])
    return r.results[0]["out_0_dram"]
```

```python
import concourse.bass as bass
from concourse import mybir
from contextlib import ExitStack


def gnn_layer_program(nc, x, adj, emb, W1, b1, W2, b2, gcn_w, gcn_b, Wo, bo, out):
    f32, f16, i32 = mybir.dt.float32, mybir.dt.float16, mybir.dt.int32
    ALU, ACT, AX = mybir.AluOpType, mybir.ActivationFunctionType, mybir.AxisListType
    ABSMAX, MAX = bass.bass_isa.ReduceOp.absmax, bass.bass_isa.ReduceOp.max

    P = 128
    GRAPHS, S, D = x.shape
    NT, DE = emb.shape
    DC = D // P
    KT = 4
    GT = P // S
    N = KT * P
    HALF = GRAPHS // GT // 2
    NSUP = GRAPHS * S // N
    EDGE = 1
    EPS = 1e-5
    HIDDEN = 2.0 ** 100

    H_SCALE = 2.0 ** 10
    W_TOP = 2.0 ** 13
    PROJ = 2.0 ** -18
    A_SCALE = 2.0 ** 14
    Z_DOWN = 2.0 ** -14
    Y_SCALE = H_SCALE * PROJ
    S_SCALE = Y_SCALE * H_SCALE
    TINY = 2.0 ** -40
    EXP_MASK = 0x7F800000
    EXP_FLIP = 254 << 23
    COEF_STEPS = 20

    TYPED = range(EDGE + 1, NT)
    x_rows = x.rearrange("(s k g) i d -> s (g i) k d", s=NSUP, k=KT, g=GT)
    out_rows = out.rearrange("(s k g) i d -> s (g i) k d", s=NSUP, k=KT, g=GT)
    adj_rows = adj.rearrange("(t g) i j -> (g i) t j", g=GT)

    ctx = ExitStack()
    with ctx:
        def sb(name, shape, dt=f32):
            return ctx.enter_context(nc.sbuf_tensor(name, shape, dt))

        def sem(name):
            return ctx.enter_context(nc.semaphore(name))

        w1_dep = sb("w1_dep", [DE, D])
        w2_dep = sb("w2_dep", [DE, D])
        e_col = sb("e_col", [DE, 1])
        b1_col = sb("b1_col", [P, DC])
        b2_col = sb("b2_col", [P, DC])
        p_col = sb("p_col", [P, DC])
        q_col = sb("q_col", [P, DC])
        pq_col = sb("pq_col", [P, DC])
        hidden = sb("hidden", [P, S])
        pair_vec = sb("pair_vec", [P, 2, DC])
        pq_all = sb("pq_all", [P, 1])
        gcn_raw = sb("gcn_raw", [P, DC, D + 1])
        wo_raw = sb("wo_raw", [P, DC, D])
        bo_all = sb("bo_all", [P, 1, D])
        ident = sb("ident", [P, P])
        ones = sb("ones", [P, P])
        peak_part = sb("peak_part", [P, DC + 3])
        peak_all = sb("peak_all", [P, DC + 3])
        peak = sb("peak", [P, 3])
        peak_bits = sb("peak_bits", [P, 3], i32)
        top_type = sb("top_type", [P, 2])
        top_all = sb("top_all", [P, 2])
        top_one = sb("top_one", [P, 1])
        has_types = sb("has_types", [P, 1], i32)
        flip_bits = sb("flip_bits", [P, 3], i32)
        unscale = sb("unscale", [P, 3])
        scale = sb("scale", [P, 3])
        warm = sb("warm", [P, 1])
        exp_scale = sb("exp_scale", [P, 1])
        exp_nscale = sb("exp_nscale", [P, 1])
        out_scale = sb("out_scale", [P, 1])
        out_half = sb("out_half", [P, 1])
        pair_bias = sb("pair_bias", [P, DC])
        pq_scaled = sb("pq_scaled", [P, 1])
        gcn_bias = sb("gcn_bias", [P, DC])
        m_hi = sb("m_hi", [P, DC, D], f16)
        m_lo = sb("m_lo", [P, DC, D], f16)
        gw_hi = sb("gw_hi", [P, DC, D + 1], f16)
        gw_lo = sb("gw_lo", [P, DC, D + 1], f16)
        wo_hi = sb("wo_hi", [P, DC, D], f16)
        wo_lo = sb("wo_lo", [P, DC, D], f16)

        x_all = sb("x_all", [P, NSUP, KT, D])
        adj_all = sb("adj_all", [P, NSUP * KT, S], i32)[:, :, :]
        bias_all = adj_all.bitcast(f32)
        w1_raw, w2_raw, w1T, w2T = (x_all[:, NSUP - 4 + n, 0:DC, :] for n in range(4))
        m_raw = w1_raw
        stats6 = sb("stats6", [P, KT, 6])
        var_d = sb("var_d", [P, KT])[:, :]
        root = sb("root", [P, KT])[:, :]
        root_sq = sb("root_sq", [P, KT])[:, :]
        const_values = {"spread": D / 4, "d_eps": D * EPS, "minus_half": -0.5, "three_halves": 1.5,
                        "h_scale": H_SCALE * D ** 0.5}
        const_all = sb("const_all", [P, len(const_values), KT])
        const = {name: const_all[:, n, :] for n, name in enumerate(const_values)}
        ln_mul = sb("ln_mul", [P, KT])[:, :]
        ln_add = sb("ln_add", [P, KT])[:, :]
        h_tok = sb("h_tok", [P, KT, D])
        hT_hi = sb("hT_hi", [P, DC, N], f16)
        hT_lo = sb("hT_lo", [P, DC, N], f16)
        g32 = sb("g32", [P, DC, N])
        g_hi = sb("g_hi", [P, DC, N], f16)
        g_lo = sb("g_lo", [P, DC, N], f16)
        hg_hi = sb("hg_hi", [P, KT, D], f16)
        hg_lo = sb("hg_lo", [P, KT, D], f16)
        row_term = sb("row_term", [P, KT])
        edge_bias = sb("edge_bias", [P, KT, P])
        scores = sb("scores", [P, KT, P])
        row_max = sb("row_max", [P, KT])
        exp_bias = sb("exp_bias", [P, KT])
        row_sum = sb("row_sum", [P, KT])
        row_inv = sb("row_inv", [P, KT])
        att = sb("att", [P, KT, P])
        attT_hi = sb("attT_hi", [P, N], f16)
        attT_lo = sb("attT_lo", [P, N], f16)
        z32 = sb("z32", [P, DC, N])
        z_hi = sb("z_hi", [P, DC, N], f16)
        z_lo = sb("z_lo", [P, DC, N], f16)

        ty_x, ty_h, ty_hT_flat, ty_misc = (x_all[:, NSUP - 8 + n, :, :].rearrange("p k d -> p (k d)")
                                           for n in range(4))
        ty_x = ty_x.rearrange("p (k d) -> p k d", k=KT)
        ty_h = ty_h.rearrange("p (k d) -> p k d", k=KT)
        ty_hT = ty_hT_flat.rearrange("p (c n) -> p c n", c=DC)
        ty_stage = ty_misc[:, 0:DC * P].rearrange("p (c n) -> p c n", c=DC)
        ty_equal = ty_misc[:, DC * P:DC * P + KT * S].rearrange("p (k j) -> p k j", k=KT)
        ty_term = ty_misc[:, DC * P + KT * S:DC * P + 2 * KT * S].rearrange("p (k j) -> p k j", k=KT)
        ty_types = ty_misc[:, DC * P + 2 * KT * S:DC * P + 3 * KT * S].bitcast(i32)\
                   .rearrange("p (k j) -> p k j", k=KT)
        ty_emb = sb("ty_emb", [NT, DE])
        ty_embT = sb("ty_embT", [DE, NT])
        ty_pT = sb("ty_pT", [P, DC, NT])
        ty_qT = sb("ty_qT", [P, DC, NT])
        ty_pqT = sb("ty_pqT", [P, DC, NT])
        ty_vec = sb("ty_vec", [P, 2, DC, NT])
        ty_pq = sb("ty_pq", [P, NT])
        ty_value = sb("ty_value", [P, NT])
        ty_row = sb("ty_row", [P, KT, NT])
        ty_stats6 = sb("ty_stats6", [P, KT, 6])
        ty_ln_mul = sb("ty_ln_mul", [P, KT])[:, :]
        ty_ln_add = sb("ty_ln_add", [P, KT])[:, :]

        bank = [ctx.enter_context(nc.psum_tensor(f"bank{i}", [P, 512], f32)) for i in range(8)]
        G_BANK, Z_BANK, HG_BANK, T_BANK, O_BANK = (0, 1, 2), (3, 4, 5), (0, 1, 2, 3), (4, 5, 0), (1, 2, 3, 4)
        score_bank, attT_bank = bank[6], bank[7]

        names = """w1_loaded w2_loaded dep_loaded gcn_loaded wo_loaded bo_loaded adj_loaded adj_rest_loaded b_loaded gcn_b_loaded x_loaded
            ident_zeroed ident_made ones_made cross_hidden w_transposed w_copied
            pq_projected pq_biased pq_multiplied m_done vectors_done m_copied vectors_copied
            weight_peaks m_peaks weight_peaks_all m_peaks_all scale_step weight_scales_ready m_scale_ready
            m_high m_split gw_high gw_split gw_vector wo_high wo_split first_rows_done
            top_types top_types_all types_known
            consts_made bias_made stats_ready coef_ready h_ready
            t_done t_high t_split g_done g_copied g_high g_split hg_done hg_high hg_split
            s_done edge_ready scored maxed exp_bias_ready exp_done inverted att_ready
            attT_done attT_high attT_split z_done z_copied z_high z_split o_done o_added x_biased stored
            ty_emb_loaded ty_pe_setup ty_dve_setup ty_free ty_loaded ty_stats_ready ty_coef_ready ty_h_ready
            ty_t_done ty_hT_ready ty_rows_done ty_rows_ready ty_staged ty_column_done ty_dve_step ty_equal_done ty_term_done ty_added ty_base_made row_ready""".split()
        sems = {n: sem(n) for n in names}
        (w1_loaded, w2_loaded, dep_loaded, gcn_loaded, wo_loaded, bo_loaded, adj_loaded, adj_rest_loaded, b_loaded, gcn_b_loaded, x_loaded,
         ident_zeroed, ident_made, ones_made, cross_hidden, w_transposed, w_copied, pq_projected, pq_biased,
         pq_multiplied, m_done, vectors_done, m_copied, vectors_copied, weight_peaks, m_peaks,
         weight_peaks_all, m_peaks_all, scale_step, weight_scales_ready, m_scale_ready, m_high, m_split,
         gw_high, gw_split, gw_vector, wo_high, wo_split, first_rows_done, top_types, top_types_all,
         types_known, consts_made, bias_made, stats_ready, coef_ready, h_ready, t_done, t_high, t_split,
         g_done, g_copied, g_high, g_split, hg_done, hg_high, hg_split, s_done, edge_ready, scored, maxed,
         exp_bias_ready, exp_done, inverted, att_ready, attT_done, attT_high, attT_split, z_done, z_copied,
         z_high, z_split, o_done, o_added, x_biased, stored, ty_emb_loaded, ty_pe_setup, ty_dve_setup, ty_free,
         ty_loaded, ty_stats_ready, ty_coef_ready, ty_h_ready, ty_t_done, ty_hT_ready, ty_rows_done,
         ty_rows_ready, ty_staged, ty_column_done, ty_dve_step,
         ty_equal_done, ty_term_done, ty_added, ty_base_made, row_ready) = [sems[n] for n in names]

        block = ctx.enter_context(nc.Block())
        LAST = NSUP - 1
        SC_M, SC_WO, SC_GCN = 0, 1, 2

        def typed(eng):
            eng.wait_ge(types_known, 1)
            return eng.If(eng.value_load(has_types[0:1, 0:1], min_val=0, max_val=1))

        @block.sync
        def _(sp):
            def load_x(s):
                sp.dma_start(x_all[:, s, :, :], x_rows[s, :, :, :]).then_inc(x_loaded, 16)

            def store_out(s):
                sp.wait_ge(o_added, KT * (s + 1))
                sp.dma_start(out_rows[s, :, :, :], x_all[:, s, :, :]).then_inc(stored, 16)

            sp.dma_start(w1_raw, W1[0:D, :].rearrange("(c p) e -> p c e", p=P)).then_inc(w1_loaded, 16)
            load_x(0)
            sp.dma_start(gcn_raw[:, :, 0:D], gcn_w.rearrange("(c p) e -> p c e", p=P)).then_inc(gcn_loaded, 16)
            sp.dma_start(b1_col[:, :], b1.rearrange("(c p) -> p c", p=P),
                         allow_slow_non_contiguous=True).then_inc(b_loaded, 16)
            sp.dma_start(b2_col[:, :], b2.rearrange("(c p) -> p c", p=P),
                         allow_slow_non_contiguous=True).then_inc(b_loaded, 16)
            sp.dma_start(gcn_raw[:, :, D:D + 1], gcn_b.rearrange("(c p o) -> p c o", p=P, o=1),
                         allow_slow_non_contiguous=True).then_inc(gcn_b_loaded, 16)
            sp.dma_start(adj_all[:, 0:HALF, :], adj_rows[:, 0:HALF, :]).then_inc(adj_loaded, 16)
            sp.dma_start(wo_raw[:, :, :], Wo.rearrange("(c p) e -> p c e", p=P)).then_inc(wo_loaded, 16)
            sp.dma_start(adj_all[:, HALF:, :], adj_rows[:, HALF:, :]).then_inc(adj_rest_loaded, 16)
            for s in range(1, 4):
                sp.wait_ge(x_loaded, 16 * s)
                load_x(s)

            with typed(sp):
                sp.dma_start(ty_emb[:, :], emb).then_inc(ty_emb_loaded, 16)
                with sp.Fori(0, NSUP) as s:
                    sp.wait_ge(ty_free, s + 1)
                    sp.dma_start(ty_x, x_rows[s, :, :, :]).then_inc(ty_loaded, 16)
                    sp.dma_start(ty_types, adj_rows[:, bass.ds(KT * s, KT), :]).then_inc(ty_loaded, 16)
                sp.wait_ge(ty_free, NSUP + 1)

            with sp.Fori(0, NSUP - 4) as s:
                sp.wait_ge(x_loaded, 16 * (s + 4))
                load_x(s + 4)
                store_out(s)
            with sp.Fori(NSUP - 4, LAST) as s:
                store_out(s)
            for k in range(KT):
                sp.wait_ge(o_added, KT * LAST + k + 1)
                sp.dma_start(out_rows[LAST, :, k, :], x_all[:, LAST, k, :]).then_inc(stored, 16)
            sp.wait_ge(stored, 16 * (LAST + KT))

        @block.gpsimd
        def _(pool):
            nc.gpsimd.memset(ident[:, :], 0.0).then_inc(ident_zeroed, 1)
            nc.gpsimd.memset(ones[:, :], 1.0).then_inc(ones_made, 1)
            nc.gpsimd.memset(edge_bias[:, :, :], -2 * HIDDEN).then_inc(cross_hidden, 1)
            pool.wait_ge(ident_zeroed, 1)
            nc.gpsimd.affine_select(out=ident[:, :], in_=ident[:, :], compare_op=ALU.not_equal, fill=1.0,
                                    base=0, pattern=[[-1, P]], channel_multiplier=1).then_inc(ident_made, 1)

            def coefficients(s, stats, mul, add, counted):
                mean_e, mean_o, m2_e, m2_o = (stats[:, :, n] for n in (1, 4, 2, 5))
                done = 0

                def step(dst, in0, in1, op):
                    nonlocal done
                    if done:
                        pool.wait_ge(counted, COEF_STEPS * s + done)
                    nc.gpsimd.tensor_tensor(dst, in0, in1, op).then_inc(counted, 1)
                    done += 1

                step(root_sq, mean_e, mean_o, ALU.subtract)
                step(root_sq, root_sq, root_sq, ALU.mult)
                step(root_sq, root_sq, const["spread"], ALU.mult)
                step(var_d, m2_e, m2_o, ALU.add)
                step(var_d, var_d, root_sq, ALU.add)
                step(var_d, var_d, const["d_eps"], ALU.add)
                step(root, var_d, const["minus_half"], ALU.pow)
                step(var_d, var_d, const["minus_half"], ALU.mult)
                for _ in range(2):
                    step(root_sq, root, root, ALU.mult)
                    step(root_sq, root_sq, var_d, ALU.mult)
                    step(root_sq, root_sq, const["three_halves"], ALU.add)
                    step(root, root, root_sq, ALU.mult)
                step(mul, root, const["h_scale"], ALU.mult)
                step(root_sq, mean_e, mean_o, ALU.add)
                step(root_sq, root_sq, mul, ALU.mult)
                step(add, root_sq, const["minus_half"], ALU.mult)
                assert done == COEF_STEPS

            def main_coefficients(s):
                pool.wait_ge(stats_ready, s + 1)
                if not isinstance(s, int) or s >= 1:
                    pool.wait_ge(h_ready, s)
                coefficients(s, stats6, ln_mul, ln_add, coef_ready)

            def edge_masks(s):
                for g in range(GT):
                    rows = slice(g * S, (g + 1) * S)
                    nc.gpsimd.tensor_tensor(edge_bias[rows, :, g * S:(g + 1) * S],
                                            bias_all[rows, bass.ds(KT * s, KT), :],
                                            hidden[rows, :].unsqueeze(1).broadcast_to([S, KT, S]),
                                            ALU.mult).then_inc(edge_ready, 1)
                pool.wait_ge(edge_ready, GT * (s + 1))

            pool.dma_start(bo_all[:, 0, :], bo.partition_broadcast(P)).then_inc(bo_loaded, 16)
            def g_low_parts(s):
                for c in range(DC):
                    pool.wait_ge(g_high, DC * s + c + 1)
                    nc.gpsimd.tensor_tensor(g_lo[:, c, :], g32[:, c, :], g_hi[:, c, :],
                                            ALU.subtract).then_inc(g_split, 1)

            for n, value in enumerate(const_values.values()):
                nc.gpsimd.memset(const_all[:, n, :], value)
            ins = nc.gpsimd.memset(hidden[:, :], HIDDEN)
            ins.then_inc(consts_made, 1)
            pool.wait_ge(consts_made, 1)
            pool.wait_ge(cross_hidden, 1)
            pool.wait_ge(weight_peaks, 1)
            nc.gpsimd.partition_all_reduce(peak_all[:, DC + 2:DC + 3], peak_part[:, DC + 2:DC + 3], P,
                                           ABSMAX).then_inc(weight_peaks_all, 1)
            main_coefficients(0)
            main_coefficients(1)
            pool.wait_ge(m_peaks, DC + 2)
            nc.gpsimd.partition_all_reduce(peak_all[:, 0:DC + 2], peak_part[:, 0:DC + 2], P,
                                           ABSMAX).then_inc(m_peaks_all, 1)
            pool.wait_ge(top_types, 2)
            nc.gpsimd.partition_all_reduce(top_all[:, :], top_type[:, :], P, MAX).then_inc(top_types_all, 1)
            nc.gpsimd.tensor_scalar(bias_all[:, :, :], adj_all[:, :, :], -float(EDGE), 1.0,
                                    ALU.add, ALU.mult).then_inc(bias_made, 1)
            pool.wait_ge(bias_made, 1)
            g_low_parts(0)

            with typed(pool):
                with pool.Fori(0, NSUP) as s:
                    pool.wait_ge(ty_stats_ready, s + 1)
                    coefficients(s, ty_stats6, ty_ln_mul, ty_ln_add, ty_coef_ready)
                pool.wait_ge(ty_free, NSUP + 1)

            pool.wait_ge(g_split, DC)
            edge_masks(0)
            pool.wait_ge(bo_loaded, 16)

            def iteration(s, prev=True, cur=True, nxt=True, nxt2=True):
                if cur and prev:
                    g_low_parts(s)
                if prev:
                    for c in range(DC):
                        pool.wait_ge(z_high, DC * (s - 1) + c + 1)
                        nc.gpsimd.tensor_tensor(z_lo[:, c, :], z32[:, c, :], z_hi[:, c, :],
                                                ALU.subtract).then_inc(z_split, 1)
                if nxt2:
                    main_coefficients(s + 2)
                if cur:
                    pool.wait_ge(h_ready, s + 1)
                    nc.gpsimd.tensor_tensor(x_all[:, s, :, :], x_all[:, s, :, :],
                                            bo_all[:, :, :].broadcast_to([P, KT, D]),
                                            ALU.add).then_inc(x_biased, 1)
                if nxt:
                    pool.wait_ge(scored, KT * (s + 1))
                    pool.wait_ge(x_biased, s + 1)
                    edge_masks(s + 1)

            iteration(0, prev=False)
            iteration(1)
            with pool.Fori(2, LAST - 1) as s:
                iteration(s)
            iteration(LAST - 1, nxt2=False)
            iteration(LAST, nxt=False, nxt2=False)
            iteration(LAST + 1, cur=False, nxt=False, nxt2=False)

        @block.scalar
        def _(act):
            act.dma_start(w2_raw, W2[0:D, :].rearrange("(c p) e -> p c e", p=P)).then_inc(w2_loaded, 16)
            act.dma_start(e_col[:, :], emb[EDGE, :].rearrange("(k o) -> k o", o=1)).then_inc(dep_loaded, 16)
            act.dma_start(w1_dep[:, :], W1[D:D + DE, :]).then_inc(dep_loaded, 16)
            act.dma_start(w2_dep[:, :], W2[D:D + DE, :]).then_inc(dep_loaded, 16)
            act.wait_ge(ones_made, 1)
            nc.scalar.activation(warm[:, :], ones[:, 0:1], ACT.Exp)

            def normalise(s):
                act.wait_ge(coef_ready, COEF_STEPS * (s + 1))
                if not isinstance(s, int) or s >= 1:
                    act.wait_ge(t_done, DC * s)
                for k in range(KT):
                    ins = nc.scalar.activation(h_tok[:, k, :], x_all[:, s, k, :], ACT.Relu,
                                               bias=ln_add[:, k:k + 1], scale=ln_mul[:, k:k + 1])
                ins.then_inc(h_ready, 1)

            def transposed_high(s):
                if not isinstance(s, int) or s >= 1:
                    act.wait_ge(s_done, s)
                for c in range(DC):
                    act.wait_ge(t_done, DC * s + c + 1)
                    nc.scalar.activation(hT_hi[:, c, :], bank[T_BANK[c]][:, :], ACT.Copy).then_inc(t_high, 1)

            def g_chunk_out(s, c):
                act.wait_ge(g_done, DC * s + c + 1)
                nc.scalar.activation(g32[:, c, :], bank[G_BANK[c]][:, :], ACT.Identity,
                                     bias=pair_bias[:, c:c + 1], scale=PROJ).then_inc(g_copied, 1)

            def hg_high_part(s, k):
                act.wait_ge(hg_done, KT * s + k + 1)
                nc.scalar.activation(hg_hi[:, k, :], bank[HG_BANK[k]][:, 0:D], ACT.Copy,
                                     scale=PROJ).then_inc(hg_high, 1)

            for c in range(DC):
                act.wait_ge(w_transposed, c + 1)
                nc.scalar.activation(w1T[:, c, :], bank[c][:, 0:D], ACT.Copy).then_inc(w_copied, 1)
            normalise(0)
            act.wait_ge(weight_scales_ready, 1)
            nc.scalar.activation(gw_hi[:, :, 0:D], gcn_raw[:, :, 0:D], ACT.Copy,
                                 scale=scale[:, SC_GCN:SC_GCN + 1]).then_inc(gw_high, 1)
            for c in range(DC):
                act.wait_ge(m_done, c + 1)
                nc.scalar.activation(m_raw[:, c, :], bank[c][:, 0:D], ACT.Copy).then_inc(m_copied, 1)
            transposed_high(0)
            act.wait_ge(m_scale_ready, 1)
            for c in range(DC):
                nc.scalar.activation(m_hi[:, c, :], m_raw[:, c, :], ACT.Copy,
                                     scale=scale[:, SC_M:SC_M + 1]).then_inc(m_high, 1)
            nc.scalar.activation(gw_hi[:, :, D], pair_vec[:, 1, :], ACT.Copy,
                                 scale=scale[:, SC_M:SC_M + 1]).then_inc(gw_high, 1)
            for k in range(KT):
                hg_high_part(0, k)
            for c in range(DC):
                g_chunk_out(0, c)
            normalise(1)
            nc.scalar.activation(wo_hi[:, :, :], wo_raw[:, :, :], ACT.Copy,
                                 scale=scale[:, SC_WO:SC_WO + 1]).then_inc(wo_high, 1)

            with typed(act):
                with act.Fori(0, NSUP) as s:
                    act.wait_ge(ty_coef_ready, COEF_STEPS * (s + 1))
                    for k in range(KT):
                        ins = nc.scalar.activation(ty_h[:, k, :], ty_x[:, k, :], ACT.Relu,
                                                   bias=ty_ln_add[:, k:k + 1], scale=ty_ln_mul[:, k:k + 1])
                    ins.then_inc(ty_h_ready, 1)
                act.wait_ge(ty_free, NSUP + 1)

            def iteration(s, prev=True, prev2=True, cur=True, nxt=True, nxt2=True):
                for c in range(DC):
                    if cur and prev:
                        act.wait_ge(g_split, DC * (s - 1) + c + 1)
                        g_chunk_out(s, c)
                    if c == 0 and prev:
                        act.wait_ge(attT_done, s)
                        if prev2:
                            act.wait_ge(z_done, DC * (s - 1))
                        nc.scalar.activation(attT_hi[:, :], attT_bank[:, :], ACT.Copy,
                                             scale=A_SCALE).then_inc(attT_high, 1)
                if prev:
                    for c in range(DC):
                        act.wait_ge(z_done, DC * (s - 1) + c + 1)
                        if prev2:
                            act.wait_ge(z_split, DC * (s - 2) + c + 1)
                        nc.scalar.activation(z32[:, c, :], bank[Z_BANK[c]][:, :], ACT.Relu,
                                             bias=gcn_bias[:, c:c + 1], scale=Z_DOWN).then_inc(z_copied, 1)
                if cur and prev:
                    act.wait_ge(z_done, DC * s)
                    for k in range(KT):
                        hg_high_part(s, k)
                if nxt:
                    transposed_high(s + 1)
                if cur:
                    act.wait_ge(exp_bias_ready, s + 1)
                    for k in range(KT):
                        nc.scalar.activation(scores[:, k, :], scores[:, k, :], ACT.Exp,
                                             bias=exp_bias[:, k:k + 1], scale=exp_scale[:, 0:1],
                                             accum_out=row_sum[:, k:k + 1]).then_inc(exp_done, 1)
                if nxt2:
                    normalise(s + 2)

            iteration(0, prev=False, prev2=False)
            iteration(1, prev2=False)
            with act.Fori(2, LAST - 1) as s:
                iteration(s)
            iteration(LAST - 1, nxt2=False)
            iteration(LAST, nxt=False, nxt2=False)
            iteration(LAST + 1, cur=False, nxt=False, nxt2=False)

        @block.vector
        def _(dve):
            def statistics(s):
                dve.wait_ge(x_loaded, 16 * (s + 1))
                if not isinstance(s, int) or s >= 1:
                    dve.wait_ge(coef_ready, COEF_STEPS * s)
                for k in range(KT):
                    ins = nc.vector.bn_stats(stats6[:, k, :], x_all[:, s, k, :])
                ins.then_inc(stats_ready, 1)

            def transposed_low(s):
                for c in range(DC):
                    dve.wait_ge(t_high, DC * s + c + 1)
                    nc.vector.tensor_tensor(hT_lo[:, c, :], bank[T_BANK[c]][:, :], hT_hi[:, c, :],
                                            ALU.subtract).then_inc(t_split, 1)

            def magnitude(col, tensor, axis, counted):
                nc.vector.tensor_reduce(peak_part[:, col:col + 1], tensor, axis, ALU.max,
                                        apply_absolute_value=True).then_inc(counted, 1)

            def scales(lo, hi, base):
                dve.wait_ge(scale_step, base)
                nc.vector.tensor_scalar(peak_bits[:, lo:hi], peak[:, lo:hi].bitcast(i32), EXP_MASK, None,
                                        ALU.bitwise_and).then_inc(scale_step, 1)
                dve.wait_ge(scale_step, base + 1)
                nc.vector.tensor_scalar(flip_bits[:, lo:hi], peak_bits[:, lo:hi], -1.0, float(EXP_FLIP),
                                        ALU.mult, ALU.add).then_inc(scale_step, 1)
                nc.vector.tensor_scalar(unscale[:, lo:hi], peak_bits[:, lo:hi].bitcast(f32), 1.0 / W_TOP, None,
                                        ALU.mult).then_inc(scale_step, 1)
                dve.wait_ge(scale_step, base + 3)
                nc.vector.tensor_scalar(scale[:, lo:hi], flip_bits[:, lo:hi].bitcast(f32), W_TOP, None,
                                        ALU.mult).then_inc(scale_step, 1)
                dve.wait_ge(scale_step, base + 4)

            def low_part(low, raw, high, col):
                return nc.vector.scalar_tensor_tensor(low, raw, scale[:, col:col + 1], high,
                                                      ALU.mult, ALU.subtract)

            for c in range(DC):
                dve.wait_ge(w_transposed, DC + c + 1)
                nc.vector.tensor_copy(w2T[:, c, :], bank[3 + c][:, 0:D]).then_inc(w_copied, 1)
            statistics(0)
            dve.wait_ge(gcn_loaded, 16)
            dve.wait_ge(gcn_b_loaded, 16)
            magnitude(DC + 2, gcn_raw[:, :, :], AX.XY, weight_peaks)
            dve.wait_ge(pq_projected, 1)
            dve.wait_ge(b_loaded, 32)
            nc.vector.tensor_tensor(p_col[:, :], bank[7][:, 0:DC], b1_col[:, :], ALU.add).then_inc(pq_biased, 1)
            nc.vector.tensor_tensor(q_col[:, :], bank[7][:, DC:2 * DC], b2_col[:, :], ALU.add).then_inc(pq_biased, 1)
            dve.wait_ge(pq_biased, 2)
            nc.vector.tensor_tensor(pq_col[:, :], p_col[:, :], q_col[:, :], ALU.mult).then_inc(pq_multiplied, 1)
            dve.wait_ge(weight_peaks_all, 1)
            nc.vector.tensor_scalar(peak[:, SC_GCN:SC_GCN + 1], peak_all[:, DC + 2:DC + 3], TINY, None,
                                    ALU.max).then_inc(scale_step, 1)
            scales(SC_GCN, SC_GCN + 1, 1)
            nc.vector.tensor_scalar(gcn_bias[:, :], gcn_raw[:, :, D], scale[:, SC_GCN:SC_GCN + 1], Y_SCALE,
                                    ALU.mult, ALU.mult).then_inc(weight_scales_ready, 1)
            dve.wait_ge(adj_loaded, 16)
            nc.vector.tensor_reduce(top_type[:, 0:1], adj_all[:, 0:HALF, :], AX.XY, ALU.max).then_inc(top_types, 1)
            dve.wait_ge(wo_loaded, 16)
            magnitude(DC + 1, wo_raw[:, :, :], AX.XY, m_peaks)
            statistics(1)
            dve.wait_ge(gw_high, 1)
            low_part(gw_lo[:, :, 0:D], gcn_raw[:, :, 0:D], gw_hi[:, :, 0:D], SC_GCN).then_inc(gw_split, 1)
            for c in range(DC):
                dve.wait_ge(m_copied, c + 1)
                magnitude(c, m_raw[:, c, :], AX.X, m_peaks)
            transposed_low(0)
            dve.wait_ge(vectors_done, 1)
            nc.vector.tensor_copy(pair_vec[:, :, :],
                                  bank[6][:, 0:2 * DC].rearrange("p (n c) -> p n c", n=2)).then_inc(vectors_copied, 1)
            nc.vector.tensor_copy(pq_all[:, :], bank[6][:, 2 * DC:2 * DC + 1]).then_inc(vectors_copied, 1)
            dve.wait_ge(vectors_copied, 2)
            magnitude(DC, pair_vec[:, :, :], AX.XY, m_peaks)
            dve.wait_ge(m_peaks_all, 1)
            nc.vector.tensor_reduce(peak[:, SC_M:SC_M + 1], peak_all[:, 0:DC + 1], AX.X, ALU.max)\
              .then_inc(scale_step, 1)
            nc.vector.tensor_scalar(peak[:, SC_WO:SC_WO + 1], peak_all[:, DC + 1:DC + 2], TINY, None,
                                    ALU.max).then_inc(scale_step, 1)
            dve.wait_ge(scale_step, 7)
            nc.vector.tensor_scalar(peak[:, SC_M:SC_M + 1], peak[:, SC_M:SC_M + 1], TINY, None,
                                    ALU.max).then_inc(scale_step, 1)
            scales(SC_M, SC_WO + 1, 8)
            nc.vector.tensor_scalar(exp_scale[:, :], unscale[:, SC_M:SC_M + 1], 1.0 / S_SCALE, None, ALU.mult)
            nc.vector.tensor_scalar(pair_bias[:, :], pair_vec[:, 0, :], scale[:, SC_M:SC_M + 1], Y_SCALE,
                                    ALU.mult, ALU.mult).then_inc(m_scale_ready, 1)
            nc.vector.tensor_scalar(exp_nscale[:, :], unscale[:, SC_M:SC_M + 1], -1.0 / S_SCALE, None, ALU.mult)
            nc.vector.tensor_scalar(pq_scaled[:, :], pq_all[:, :], scale[:, SC_M:SC_M + 1], S_SCALE,
                                    ALU.mult, ALU.mult)
            nc.vector.tensor_scalar(out_half[:, :], unscale[:, SC_GCN:SC_GCN + 1], 1.0 / Y_SCALE, None,
                                    ALU.mult).then_inc(scale_step, 1)
            dve.wait_ge(scale_step, 13)
            nc.vector.tensor_scalar(out_scale[:, :], out_half[:, :], unscale[:, SC_WO:SC_WO + 1], None,
                                    ALU.mult).then_inc(scale_step, 1)
            for c in range(DC):
                dve.wait_ge(m_high, c + 1)
                low_part(m_lo[:, c, :], m_raw[:, c, :], m_hi[:, c, :], SC_M).then_inc(m_split, 1)
            dve.wait_ge(gw_high, 2)
            low_part(gw_lo[:, :, D], pair_vec[:, 1, :], gw_hi[:, :, D], SC_M).then_inc(gw_vector, 1)
            dve.wait_ge(adj_rest_loaded, 16)
            nc.vector.tensor_reduce(top_type[:, 1:2], adj_all[:, HALF:, :], AX.XY, ALU.max).then_inc(top_types, 1)

            def hg_low_part(s, k):
                dve.wait_ge(hg_high, KT * s + k + 1)
                nc.vector.scalar_tensor_tensor(hg_lo[:, k, :], bank[HG_BANK[k]][:, 0:D], PROJ,
                                               hg_hi[:, k, :], ALU.mult, ALU.subtract).then_inc(hg_split, 1)

            def g_high_part(s, c):
                dve.wait_ge(g_copied, DC * s + c + 1)
                nc.vector.tensor_copy(g_hi[:, c, :], g32[:, c, :]).then_inc(g_high, 1)

            for k in range(KT):
                hg_low_part(0, k)
            dve.wait_ge(top_types_all, 1)
            nc.vector.tensor_reduce(top_one[:, :], top_all[:, :], AX.X, ALU.max).then_inc(top_types, 1)
            dve.wait_ge(top_types, 3)
            nc.vector.tensor_scalar(has_types[:, :], top_one[:, :], float(EDGE), None,
                                    ALU.is_gt).then_inc(types_known, 1)
            for c in range(DC):
                g_high_part(0, c)
            dve.wait_ge(wo_high, 1)
            low_part(wo_lo[:, :, :], wo_raw[:, :, :], wo_hi[:, :, :], SC_WO).then_inc(wo_split, 1)

            with typed(dve):
                dve.wait_ge(ty_pe_setup, 1)
                nc.vector.tensor_copy(ty_embT[:, :], bank[4][0:DE, 0:NT]).then_inc(ty_dve_setup, 1)
                dve.wait_ge(ty_pe_setup, 2)
                for n, (vT, b_col) in enumerate(((ty_pT, b1_col), (ty_qT, b2_col))):
                    for c in range(DC):
                        at = (n * DC + c) * NT
                        nc.vector.tensor_scalar(vT[:, c, :], bank[5][:, at:at + NT], b_col[:, c:c + 1], None,
                                                ALU.add).then_inc(ty_dve_step, 1)
                dve.wait_ge(ty_dve_step, 2 * DC)
                nc.vector.tensor_tensor(ty_pqT[:, :, :], ty_pT[:, :, :], ty_qT[:, :, :],
                                        ALU.mult).then_inc(ty_dve_setup, 1)
                dve.wait_ge(ty_pe_setup, 3)
                for n in range(2):
                    for c in range(DC):
                        at = (n * DC + c) * NT
                        nc.vector.tensor_scalar(ty_vec[:, n, c, :], bank[6][:, at:at + NT],
                                                pair_vec[:, n, c:c + 1], scale[:, SC_M:SC_M + 1],
                                                ALU.subtract, ALU.mult).then_inc(ty_dve_step, 1)
                nc.vector.tensor_scalar(ty_pq[:, :], bank[7][:, 0:NT], pq_all[:, 0:1], scale[:, SC_M:SC_M + 1],
                                        ALU.subtract, ALU.mult).then_inc(ty_dve_step, 1)
                for t in range(NT):
                    ins = nc.vector.memset(ty_value[:, t:t + 1], float(t))
                ins.then_inc(ty_dve_step, 1)
                dve.wait_ge(ty_dve_step, 4 * DC + 2)
                nc.vector.tensor_scalar(ty_vec[:, :, :, :], ty_vec[:, :, :, :], Y_SCALE, None,
                                        ALU.mult).then_inc(ty_dve_step, 1)
                nc.vector.tensor_scalar(ty_pq[:, :], ty_pq[:, :], S_SCALE, None, ALU.mult).then_inc(ty_dve_step, 1)
                dve.wait_ge(ty_dve_step, 4 * DC + 4)
                dve.wait_ge(bias_made, 1)
                nc.vector.sem_inc(ty_free, 1)
                with dve.Fori(0, NSUP) as s:
                    dve.wait_ge(ty_loaded, 32 * (s + 1))
                    nc.vector.tensor_scalar(bias_all[:, bass.ds(KT * s, KT), :], ty_types, 1.0, -1.0,
                                            ALU.min, ALU.add).then_inc(ty_base_made, 1)
                    for k in range(KT):
                        ins = nc.vector.bn_stats(ty_stats6[:, k, :], ty_x[:, k, :])
                    ins.then_inc(ty_stats_ready, 1)
                    dve.wait_ge(ty_t_done, s + 1)
                    for c in range(DC):
                        ins = nc.vector.tensor_copy(ty_hT[:, c, :], bank[4 + c][:, :])
                    ins.then_inc(ty_hT_ready, 1)
                    dve.wait_ge(ty_rows_done, s + 1)
                    nc.vector.tensor_tensor(ty_row[:, :, :],
                                            bank[7][:, 0:KT * NT].rearrange("p (k t) -> p k t", k=KT),
                                            ty_pq[:, :].unsqueeze(1).broadcast_to([P, KT, NT]),
                                            ALU.add).then_inc(ty_rows_ready, 1)
                    with dve.Fori(TYPED.start, TYPED.stop) as t:
                        n = len(TYPED) * s + t - TYPED.start
                        nc.vector.tensor_copy(ty_stage, ty_vec[:, 0, :, bass.ds(t, 1)].broadcast_to([P, DC, P]))\
                          .then_inc(ty_staged, 1)
                        nc.vector.tensor_scalar(ty_equal, ty_types, ty_value[:, bass.ds(t, 1)], None,
                                                ALU.is_equal).then_inc(ty_equal_done, 1)
                        dve.wait_ge(ty_rows_ready, s + 1)
                        dve.wait_ge(ty_base_made, s + 1)
                        dve.wait_ge(ty_column_done, n + 1)
                        dve.wait_ge(ty_equal_done, n + 1)
                        for g in range(GT):
                            rows = slice(g * S, (g + 1) * S)
                            for k in range(KT):
                                at = k * P + g * S
                                nc.vector.scalar_tensor_tensor(
                                    ty_term[rows, k, :], bank[4][rows, at:at + S], ty_row[rows, k, bass.ds(t, 1)],
                                    ty_equal[rows, k, :], ALU.add, ALU.mult).then_inc(ty_term_done, 1)
                        dve.wait_ge(ty_term_done, GT * KT * (n + 1))
                        here = bias_all[:, bass.ds(KT * s, KT), :]
                        nc.vector.scalar_tensor_tensor(here, ty_term, 1.0 / HIDDEN, here,
                                                       ALU.mult, ALU.add).then_inc(ty_added, 1)
                        dve.wait_ge(ty_added, n + 1)
                    nc.vector.sem_inc(ty_free, 1)

            def iteration(s, prev=True, prev2=True, cur=True, nxt=True, nxt2=True):
                for c in range(DC):
                    if cur and prev:
                        if c == 0:
                            dve.wait_ge(s_done, s)
                        g_high_part(s, c)
                    if c == 0 and prev:
                        dve.wait_ge(attT_high, s)
                        nc.vector.scalar_tensor_tensor(attT_lo[:, :], attT_bank[:, :], A_SCALE, attT_hi[:, :],
                                                       ALU.mult, ALU.subtract).then_inc(attT_split, 1)
                if prev:
                    for c in range(DC):
                        dve.wait_ge(z_copied, DC * (s - 1) + c + 1)
                        if prev2 and c == 0:
                            dve.wait_ge(o_done, KT * (s - 1))
                        nc.vector.tensor_copy(z_hi[:, c, :], z32[:, c, :]).then_inc(z_high, 1)
                if nxt2:
                    statistics(s + 2)
                if cur:
                    if prev:
                        for k in range(KT):
                            dve.wait_ge(hg_high, KT * s + k + 1)
                            nc.vector.tensor_scalar(row_term[:, k:k + 1], bank[HG_BANK[k]][:, D:D + 1], Y_SCALE,
                                                    pq_scaled[:, 0:1], ALU.mult, ALU.add).then_inc(row_ready, 1)
                            hg_low_part(s, k)
                    else:
                        dve.wait_ge(first_rows_done, 1)
                        nc.vector.tensor_scalar(row_term[:, :], bank[7][:, 0:KT], Y_SCALE, pq_scaled[:, 0:1],
                                                ALU.mult, ALU.add).then_inc(row_ready, KT)
                    if not prev:
                        transposed_low(1)
                    dve.wait_ge(s_done, s + 1)
                    dve.wait_ge(edge_ready, GT * (s + 1))
                    dve.wait_ge(row_ready, KT * (s + 1))
                    for k in range(KT):
                        nc.vector.scalar_tensor_tensor(scores[:, k, :], score_bank[:, k * P:(k + 1) * P],
                                                       row_term[:, k:k + 1], edge_bias[:, k, :],
                                                       ALU.add, ALU.add).then_inc(scored, 1)
                    dve.wait_ge(scored, KT * (s + 1))
                    nc.vector.tensor_reduce(row_max[:, :], scores[:, :, :], AX.X, ALU.max).then_inc(maxed, 1)
                    dve.wait_ge(maxed, s + 1)
                    nc.vector.tensor_scalar(exp_bias[:, :], row_max[:, :], exp_nscale[:, 0:1], None,
                                            ALU.mult).then_inc(exp_bias_ready, 1)
                if nxt and prev:
                    transposed_low(s + 1)
                if cur:
                    dve.wait_ge(exp_done, KT * (s + 1))
                    nc.vector.reciprocal(row_inv[:, :], row_sum[:, :]).then_inc(inverted, 1)
                    dve.wait_ge(inverted, s + 1)
                    if prev:
                        dve.wait_ge(attT_done, s)
                    nc.vector.tensor_tensor(att[:, :, :], scores[:, :, :],
                                            row_inv[:, :].unsqueeze(2).broadcast_to([P, KT, P]),
                                            ALU.mult).then_inc(att_ready, 1)
                if prev:
                    dve.wait_ge(x_biased, s)
                    for k in range(KT):
                        dve.wait_ge(o_done, KT * (s - 1) + k + 1)
                        nc.vector.scalar_tensor_tensor(x_all[:, s - 1, k, :], bank[O_BANK[k]][:, 0:D],
                                                       out_scale[:, 0:1], x_all[:, s - 1, k, :],
                                                       ALU.mult, ALU.add).then_inc(o_added, 1)

            iteration(0, prev=False, prev2=False)
            iteration(1, prev2=False)
            with dve.Fori(2, LAST - 1) as s:
                iteration(s)
            iteration(LAST - 1, nxt2=False)
            iteration(LAST, nxt=False, nxt2=False)
            iteration(LAST + 1, cur=False, nxt=False, nxt2=False)

        @block.tensor
        def _(pe):
            def split_product(dst, left, right, chunks=DC):
                last = None
                for c in range(chunks):
                    (lh, ll), (rh, rl) = left(c), right(c)
                    nc.tensor.matmul(dst, lh, rh, start=(c == 0), stop=False)
                    nc.tensor.matmul(dst, lh, rl, start=False, stop=False)
                    last = nc.tensor.matmul(dst, ll, rh, start=False, stop=(c == chunks - 1))
                return last

            pe.wait_ge(ident_made, 1)
            for n, raw, loaded in ((0, w1_raw, w1_loaded), (DC, w2_raw, w2_loaded)):
                pe.wait_ge(loaded, 16)
                for c in range(DC):
                    for d in range(DC):
                        last = nc.tensor.transpose(bank[n + c][:, d * P:(d + 1) * P],
                                                   raw[:, d, c * P:(c + 1) * P], ident[:, :])
                    last.then_inc(w_transposed, 1)
            pe.wait_ge(w_copied, 2 * DC)
            for d in range(DC):
                for c in range(DC):
                    last = nc.tensor.matmul(bank[d][:, 0:D], w1T[:, c, d * P:(d + 1) * P], w2T[:, c, :],
                                            start=(c == 0), stop=(c == DC - 1))
                last.then_inc(m_done, 1)
            def transposes(s, prev=True):
                pe.wait_ge(h_ready, s + 1)
                for c in range(DC):
                    if prev and c < 2:
                        pe.wait_ge(z_copied, DC * (s - 2) + c + 2)
                    if c == 2 and prev:
                        pe.wait_ge(hg_split, KT * (s - 1) + 1)
                    for k in range(KT):
                        last = nc.tensor.transpose(bank[T_BANK[c]][:, k * P:(k + 1) * P],
                                                   h_tok[:, k, c * P:(c + 1) * P], ident[:, :])
                    last.then_inc(t_done, 1)

            def scores_of(s):
                for k in range(KT):
                    rows = slice(k * P, (k + 1) * P)
                    last = split_product(score_bank[:, rows],
                                         lambda d: (g_hi[:, d, rows], g_lo[:, d, rows]),
                                         lambda d: (hT_hi[:, d, rows], hT_lo[:, d, rows]))
                last.then_inc(s_done, 1)

            def g_chunk(c):
                split_product(bank[G_BANK[c]][:, :],
                              lambda d: (m_hi[:, d, c * P:(c + 1) * P], m_lo[:, d, c * P:(c + 1) * P]),
                              lambda d: (hT_hi[:, d, :], hT_lo[:, d, :])).then_inc(g_done, 1)

            pe.wait_ge(dep_loaded, 16 * 3)
            for n, dep in ((0, w1_dep), (DC, w2_dep)):
                for c in range(DC):
                    last = nc.tensor.matmul(bank[7][:, n + c:n + c + 1], dep[:, c * P:(c + 1) * P],
                                            e_col[:, :], start=True, stop=True)
            last.then_inc(pq_projected, 1)
            pe.wait_ge(m_copied, DC)
            transposes(0, prev=False)
            pe.wait_ge(pq_multiplied, 1)
            pe.wait_ge(ones_made, 1)
            for n, (wT, col) in enumerate(((w2T, p_col), (w1T, q_col))):
                for d in range(DC):
                    at = n * DC + d
                    for c in range(DC):
                        nc.tensor.matmul(bank[6][:, at:at + 1], wT[:, c, d * P:(d + 1) * P], col[:, c:c + 1],
                                         start=(c == 0), stop=(c == DC - 1))
            for c in range(DC):
                last = nc.tensor.matmul(bank[6][:, 2 * DC:2 * DC + 1], ones[:, :], pq_col[:, c:c + 1],
                                        start=(c == 0), stop=(c == DC - 1))
            last.then_inc(vectors_done, 1)
            pe.wait_ge(gw_split, 1)
            pe.wait_ge(t_split, DC)
            for k in range(KT):
                rows = slice(k * P, (k + 1) * P)
                split_product(bank[HG_BANK[k]][:, 0:D],
                              lambda d: (hT_hi[:, d, rows], hT_lo[:, d, rows]),
                              lambda d: (gw_hi[:, d, 0:D], gw_lo[:, d, 0:D])).then_inc(hg_done, 1)

            for c in range(DC):
                pe.wait_ge(m_split, DC)
                pe.wait_ge(hg_split, c + 1)
                g_chunk(c)
            with typed(pe):
                pe.wait_ge(ty_emb_loaded, 16)
                nc.tensor.transpose(bank[4][0:DE, 0:NT], ty_emb[:, :], ident[0:NT, 0:NT]).then_inc(ty_pe_setup, 1)
                pe.wait_ge(ty_dve_setup, 1)
                for n, dep in ((0, w1_dep), (DC, w2_dep)):
                    for c in range(DC):
                        last = nc.tensor.matmul(bank[5][:, (n + c) * NT:(n + c + 1) * NT],
                                                dep[:, c * P:(c + 1) * P], ty_embT[:, :], start=True, stop=True)
                last.then_inc(ty_pe_setup, 1)
                pe.wait_ge(ty_dve_setup, 2)
                for n, (wT, vT) in enumerate(((w2T, ty_pT), (w1T, ty_qT))):
                    for d in range(DC):
                        at = (n * DC + d) * NT
                        for c in range(DC):
                            nc.tensor.matmul(bank[6][:, at:at + NT], wT[:, c, d * P:(d + 1) * P], vT[:, c, :],
                                             start=(c == 0), stop=(c == DC - 1))
                for c in range(DC):
                    last = nc.tensor.matmul(bank[7][:, 0:NT], ones[:, :], ty_pqT[:, c, :],
                                            start=(c == 0), stop=(c == DC - 1))
                last.then_inc(ty_pe_setup, 1)
                pe.wait_ge(ty_free, 1)
                with pe.Fori(0, NSUP) as s:
                    pe.wait_ge(ty_h_ready, s + 1)
                    for c in range(DC):
                        for k in range(KT):
                            last = nc.tensor.transpose(bank[4 + c][:, k * P:(k + 1) * P],
                                                       ty_h[:, k, c * P:(c + 1) * P], ident[:, :])
                    last.then_inc(ty_t_done, 1)
                    pe.wait_ge(ty_hT_ready, s + 1)
                    for k in range(KT):
                        for c in range(DC):
                            last = nc.tensor.matmul(bank[7][:, k * NT:(k + 1) * NT], ty_hT[:, c, k * P:(k + 1) * P],
                                                    ty_vec[:, 1, c, :], start=(c == 0), stop=(c == DC - 1))
                    last.then_inc(ty_rows_done, 1)
                    with pe.Fori(TYPED.start, TYPED.stop) as t:
                        pe.wait_ge(ty_staged, len(TYPED) * s + t - TYPED.start + 1)
                        for c in range(DC):
                            last = nc.tensor.matmul(bank[4][:, :], ty_stage[:, c, :], ty_hT[:, c, :],
                                                    start=(c == 0), stop=(c == DC - 1))
                        last.then_inc(ty_column_done, 1)
                pe.wait_ge(ty_free, NSUP + 1)

            pe.wait_ge(gw_vector, 1)
            for k in range(KT):
                rows = slice(k * P, (k + 1) * P)
                last = split_product(bank[7][:, k:k + 1],
                                     lambda d: (hT_hi[:, d, rows], hT_lo[:, d, rows]),
                                     lambda d: (gw_hi[:, d, D:D + 1], gw_lo[:, d, D:D + 1]))
            last.then_inc(first_rows_done, 1)
            pe.wait_ge(g_split, DC)
            scores_of(0)
            transposes(1, prev=False)
            pe.wait_ge(wo_split, 1)

            def iteration(s, prev2=True, cur=True, nxt=True):
                for c in range(DC):
                    if cur:
                        if c == 0:
                            pe.wait_ge(t_split, DC * (s + 1))
                        elif prev2:
                            pe.wait_ge(o_added, KT * (s - 2) + c)
                        g_chunk(c)
                    if c == 0:
                        pe.wait_ge(att_ready, s)
                        if prev2:
                            pe.wait_ge(attT_split, s - 1)
                        for k in range(KT):
                            last = nc.tensor.transpose(attT_bank[:, k * P:(k + 1) * P], att[:, k, :], ident[:, :])
                        last.then_inc(attT_done, 1)
                pe.wait_ge(attT_split, s)
                pe.wait_ge(hg_split, KT * s)
                for c in range(DC):
                    if prev2 and c < 2:
                        pe.wait_ge(o_added, KT * (s - 2) + c + 3)
                    for k in range(KT):
                        rows = slice(k * P, (k + 1) * P)
                        last = split_product(
                            bank[Z_BANK[c]][:, rows],
                            lambda _: (hg_hi[:, k, c * P:(c + 1) * P], hg_lo[:, k, c * P:(c + 1) * P]),
                            lambda _: (attT_hi[:, rows], attT_lo[:, rows]), chunks=1)
                    last.then_inc(z_done, 1)
                if cur:
                    for k in range(KT):
                        rows = slice(k * P, (k + 1) * P)
                        if k < DC:
                            pe.wait_ge(g_copied, DC * s + k + 1)
                        else:
                            pe.wait_ge(z_copied, DC * (s - 1) + 1)
                        split_product(bank[HG_BANK[k]][:, 0:D + 1],
                                      lambda d: (hT_hi[:, d, rows], hT_lo[:, d, rows]),
                                      lambda d: (gw_hi[:, d, :], gw_lo[:, d, :])).then_inc(hg_done, 1)
                    pe.wait_ge(g_split, DC * (s + 1))
                    pe.wait_ge(scored, KT * s)
                    scores_of(s)
                if nxt:
                    transposes(s + 1)
                pe.wait_ge(z_split, DC * s)
                for k in range(KT):
                    rows = slice(k * P, (k + 1) * P)
                    if not cur:
                        pe.wait_ge(o_added, KT * (s - 2) + k + 1)
                    elif k < DC:
                        pe.wait_ge(hg_split, KT * s + k + 2)
                    elif nxt:
                        pe.wait_ge(t_split, DC * (s + 1) + 1)
                    split_product(bank[O_BANK[k]][:, 0:D],
                                  lambda e: (z_hi[:, e, rows], z_lo[:, e, rows]),
                                  lambda e: (wo_hi[:, e, :], wo_lo[:, e, :])).then_inc(o_done, 1)

            iteration(1, prev2=False)
            with pe.Fori(2, LAST) as s:
                iteration(s)
            iteration(LAST, nxt=False)
            iteration(LAST + 1, cur=False, nxt=False)


_INS = ['x', 'adj', 'L0_gnn_dep_emb_table', 'L0_gnn_W1_w', 'L0_gnn_W1_b', 'L0_gnn_W2_w', 'L0_gnn_W2_b',
        'L0_gnn_gcn_w', 'L0_gnn_gcn_b', 'L0_gnn_Wo_w', 'L0_gnn_Wo_b']


def kernel(**inputs):
    import numpy as _np
    import concourse.bacc as _bacc
    from concourse import mybir as _mybir
    from concourse.bass_utils import run_bass_kernel_spmd as _run

    nc = _bacc.Bacc("TRN2", target_bir_lowering=False, num_devices=1)
    arrays, args = {}, []
    for name in _INS:
        a = _np.ascontiguousarray(inputs[name])
        arrays[f"in_{name}_dram"] = a
        args.append(nc.dram_tensor(f"in_{name}_dram", a.shape, _mybir.dt.from_np(a.dtype), kind="ExternalInput").ap())
    shape = inputs['x'].shape
    args.append(nc.dram_tensor("out_0_dram", shape, _mybir.dt.float32, kind="ExternalOutput").ap())
    gnn_layer_program(nc, *args)
    r = _run(nc, [arrays], core_ids=[0])
    return r.results[0]["out_0_dram"]
```

```python
import concourse.bass as bass
from concourse import mybir
from contextlib import ExitStack


def gnn_layer_program(nc, x, adj, emb, W1, b1, W2, b2, gcn_w, gcn_b, Wo, bo, out):
    f32, f16, i32 = mybir.dt.float32, mybir.dt.float16, mybir.dt.int32
    ALU, ACT, AX = mybir.AluOpType, mybir.ActivationFunctionType, mybir.AxisListType
    ABSMAX, MAX = bass.bass_isa.ReduceOp.absmax, bass.bass_isa.ReduceOp.max

    P = 128
    GRAPHS, S, D = x.shape
    NT, DE = emb.shape
    DC = D // P
    KT = 4
    GT = P // S
    N = KT * P
    HALF = GRAPHS // GT // 2
    NSUP = GRAPHS * S // N
    EDGE = 1
    EPS = 1e-5
    HIDDEN = 2.0 ** 100

    H_SCALE = 2.0 ** 10
    W_TOP = 2.0 ** 13
    PROJ = 2.0 ** -18
    A_SCALE = 2.0 ** 14
    Z_DOWN = 2.0 ** -14
    Y_SCALE = H_SCALE * PROJ
    S_SCALE = Y_SCALE * H_SCALE
    TINY = 2.0 ** -40
    EXP_MASK = 0x7F800000
    EXP_FLIP = 254 << 23
    COEF_STEPS = 20

    TYPED = range(EDGE + 1, NT)
    x_rows = x.rearrange("(s k g) i d -> s (g i) k d", s=NSUP, k=KT, g=GT)
    out_rows = out.rearrange("(s k g) i d -> s (g i) k d", s=NSUP, k=KT, g=GT)
    adj_rows = adj.rearrange("(t g) i j -> (g i) t j", g=GT)

    ctx = ExitStack()
    with ctx:
        def sb(name, shape, dt=f32):
            return ctx.enter_context(nc.sbuf_tensor(name, shape, dt))

        def sem(name):
            return ctx.enter_context(nc.semaphore(name))

        w1_dep = sb("w1_dep", [DE + 1, D])
        w2_dep = sb("w2_dep", [DE + 1, D])
        e_col = sb("e_col", [DE + 1, 1])
        e_wide = sb("e_wide", [DE + 1, P])
        q_row = sb("q_row", [P, D])
        product = sb("product", [P, D])
        pair_vec = sb("pair_vec", [P, 2, DC])
        pq_all = sb("pq_all", [P, 1])
        gcn_raw = sb("gcn_raw", [P, DC, D + 1])
        wo_raw = sb("wo_raw", [P, DC, D])
        bo_all = sb("bo_all", [P, 1, D])
        ident = sb("ident", [P, P])
        ident16 = sb("ident16", [P, P], f16)
        ones = sb("ones", [P, P])
        peak_part = sb("peak_part", [P, DC + 3])
        peak_all = sb("peak_all", [P, DC + 3])
        peak = sb("peak", [P, 3])
        peak_bits = sb("peak_bits", [P, 3], i32)
        QUARTERS = 4
        minus_edge = sb("minus_edge", [P, 1])
        top_type = sb("top_type", [P, QUARTERS])
        top_all = sb("top_all", [P, QUARTERS])
        top_one = sb("top_one", [P, 1])
        has_types = sb("has_types", [P, 1], i32)
        flip_bits = sb("flip_bits", [P, 3], i32)
        unscale = sb("unscale", [P, 3])
        scale = sb("scale", [P, 3])
        warm = sb("warm", [P, 1])
        exp_scale = sb("exp_scale", [P, 1])
        exp_nscale = sb("exp_nscale", [P, 1])
        out_scale = sb("out_scale", [P, 1])
        out_half = sb("out_half", [P, 1])
        pair_bias = sb("pair_bias", [P, DC])
        pq_scaled = sb("pq_scaled", [P, 1])
        gcn_bias = sb("gcn_bias", [P, DC])
        m_hi = sb("m_hi", [P, DC, D], f16)
        m_lo = sb("m_lo", [P, DC, D], f16)
        gw_hi = sb("gw_hi", [P, DC, D + 1], f16)
        gw_lo = sb("gw_lo", [P, DC, D + 1], f16)
        wo_hi = sb("wo_hi", [P, DC, D], f16)
        wo_lo = sb("wo_lo", [P, DC, D], f16)

        x_all = sb("x_all", [P, NSUP, KT, D])
        adj_all = sb("adj_all", [P, NSUP * KT, S], i32)[:, :, :]
        bias_all = adj_all.bitcast(f32)
        w1_raw, w2_raw, w1T, w2T = (x_all[:, NSUP - 4 + n, 0:DC, :] for n in range(4))
        m_raw = x_all[:, NSUP - 5, 0:DC, :]
        stats6 = sb("stats6", [P, KT, 6])
        var_d = sb("var_d", [P, KT])[:, :]
        root = sb("root", [P, KT])[:, :]
        root_sq = sb("root_sq", [P, KT])[:, :]
        const_values = {"spread": D / 4, "d_eps": D * EPS, "minus_half": -0.5, "three_halves": 1.5,
                        "h_scale": H_SCALE * D ** 0.5}
        const_all = sb("const_all", [P, len(const_values), KT])
        const = {name: const_all[:, n, :] for n, name in enumerate(const_values)}
        ln_mul = sb("ln_mul", [P, KT])[:, :]
        ln_add = sb("ln_add", [P, KT])[:, :]
        h_tok = sb("h_tok", [P, KT, D])
        hT_hi = sb("hT_hi", [P, DC, N], f16)
        hT_lo = sb("hT_lo", [P, DC, N], f16)
        g32 = sb("g32", [P, DC, N])
        g_graphs = g32[:, :, :].rearrange("p c (q i) -> p c q i", i=S)
        g_parts = sb("g_parts", [P, DC, KT * GT, 2, S], f16)
        hg_hi = sb("hg_hi", [P, KT, D], f16)
        hg_parts = sb("hg_parts", [P, KT, GT, D], f16)
        row_term = sb("row_term", [P, KT])
        score_parts = sb("score_parts", [P, 2, KT, S])
        masks = sb("masks", [P, KT, S])
        scores = sb("scores", [P, KT, S])
        row_max = sb("row_max", [P, KT])
        exp_bias = sb("exp_bias", [P, KT])
        row_sum = sb("row_sum", [P, KT])
        row_inv = sb("row_inv", [P, KT])
        att = sb("att", [P, KT, S])
        att_parts = sb("att_parts", [P, KT, 2, S], f16)
        attT_parts = sb("attT_parts", [P, KT, GT, S], f16)
        attT_hi = sb("attT_hi", [P, KT, GT, S], f16)
        z32 = sb("z32", [P, DC, N])
        z_hi = sb("z_hi", [P, DC, N], f16)
        z_lo = sb("z_lo", [P, DC, N], f16)

        excess = z32[:, :, :].rearrange("p c n -> p (c n)")[:, 0:2 * HALF // QUARTERS * S]\
                 .rearrange("p (t j) -> p t j", j=S)

        ty_x, ty_h, ty_hT_flat, ty_misc = (x_all[:, NSUP - 8 + n, :, :].rearrange("p k d -> p (k d)")
                                           for n in range(4))
        ty_x = ty_x.rearrange("p (k d) -> p k d", k=KT)
        ty_h = ty_h.rearrange("p (k d) -> p k d", k=KT)
        ty_hT = ty_hT_flat.rearrange("p (c n) -> p c n", c=DC)
        ty_stage = ty_misc[:, 0:DC * P].rearrange("p (c n) -> p c n", c=DC)
        ty_equal = ty_misc[:, DC * P:DC * P + KT * S].rearrange("p (k j) -> p k j", k=KT)
        ty_term = ty_misc[:, DC * P + KT * S:DC * P + 2 * KT * S].rearrange("p (k j) -> p k j", k=KT)
        ty_types = ty_misc[:, DC * P + 2 * KT * S:DC * P + 3 * KT * S].bitcast(i32)\
                   .rearrange("p (k j) -> p k j", k=KT)
        ty_emb = sb("ty_emb", [NT, DE])
        ty_embT = sb("ty_embT", [DE + 1, NT])
        ty_pT = sb("ty_pT", [P, DC, NT])
        ty_qT = sb("ty_qT", [P, DC, NT])
        ty_pqT = sb("ty_pqT", [P, DC, NT])
        ty_vec = sb("ty_vec", [P, 2, DC, NT])
        ty_pq = sb("ty_pq", [P, NT])
        ty_value = sb("ty_value", [P, NT])
        ty_row = sb("ty_row", [P, KT, NT])
        ty_stats6 = sb("ty_stats6", [P, KT, 6])
        ty_ln_mul = sb("ty_ln_mul", [P, KT])[:, :]
        ty_ln_add = sb("ty_ln_add", [P, KT])[:, :]

        bank = [ctx.enter_context(nc.psum_tensor(f"bank{i}", [P, 512], f32)) for i in range(8)]
        G_BANK, Z_BANK, HG_BANK, T_BANK, O_BANK = (1, 2, 0), (3, 4, 5), (1, 2, 0, 3), (4, 5, 0), (1, 2, 3, 4)
        LAST_Z_BANK = (5, 0, 6)
        score_bank = bank[6][:, :].rearrange("p (k g j) -> p k g j", k=KT, g=GT)
        attT_bank = bank[7][:, :].bitcast(f16)[:, 0:N].rearrange("p (k g i) -> p k g i", k=KT, g=GT)

        names = """w1_loaded w2_loaded dep_loaded e_one e_loaded gcn_loaded gcn_b_loaded wo_loaded bo_loaded
            adj_loaded adj_rest_loaded x_loaded
            ident_zeroed ident_made ident16_made ones_made consts_made attT_cleared
            w_transposed w_copied e_widened pq_projected q_copied dot_done m_done m_copied
            weight_peaks weight_peaks_all m_peaks m_peaks_all wo_peak wo_peak_all scale_step
            weight_scales_ready m_scale_ready wo_scale_ready
            m_high m_split gw_high gw_split gw_vector wo_high wo_split
            top_types top_types_all types_known bias_made
            stats_ready coef_ready h_ready t_done t_high t_split
            g_done g_copied g_high g_split
            hg_done hg_high hg_moved hg_split first_rows_done row_ready masked
            s_done score_copied summed scored maxed exp_bias_ready exp_done inverted weighted att_high
            att_ready
            attT_done attT_copied attT_high
            z_done z_copied z_high z_split last_z_split
            o_done x_biased o_added stored
            ty_emb_loaded ty_pe_setup ty_dve_setup ty_dve_step ty_free ty_loaded ty_base_made ty_stats_ready
            ty_coef_ready ty_h_ready ty_t_done ty_hT_ready ty_rows_done ty_rows_ready ty_staged
            ty_column_done ty_equal_done ty_term_done ty_added""".split()
        sems = {n: sem(n) for n in names}
        (w1_loaded, w2_loaded, dep_loaded, e_one, e_loaded, gcn_loaded, gcn_b_loaded, wo_loaded, bo_loaded,
         adj_loaded, adj_rest_loaded, x_loaded,
         ident_zeroed, ident_made, ident16_made, ones_made, consts_made, attT_cleared,
         w_transposed, w_copied, e_widened, pq_projected, q_copied, dot_done, m_done, m_copied,
         weight_peaks, weight_peaks_all, m_peaks, m_peaks_all, wo_peak, wo_peak_all, scale_step,
         weight_scales_ready, m_scale_ready, wo_scale_ready,
         m_high, m_split, gw_high, gw_split, gw_vector, wo_high, wo_split,
         top_types, top_types_all, types_known, bias_made,
         stats_ready, coef_ready, h_ready, t_done, t_high, t_split,
         g_done, g_copied, g_high, g_split,
         hg_done, hg_high, hg_moved, hg_split, first_rows_done, row_ready, masked,
         s_done, score_copied, summed, scored, maxed, exp_bias_ready, exp_done, inverted, weighted, att_high,
         att_ready,
         attT_done, attT_copied, attT_high,
         z_done, z_copied, z_high, z_split, last_z_split,
         o_done, x_biased, o_added, stored,
         ty_emb_loaded, ty_pe_setup, ty_dve_setup, ty_dve_step, ty_free, ty_loaded, ty_base_made, ty_stats_ready,
         ty_coef_ready, ty_h_ready, ty_t_done, ty_hT_ready, ty_rows_done, ty_rows_ready, ty_staged,
         ty_column_done, ty_equal_done, ty_term_done, ty_added) = [sems[n] for n in names]

        block = ctx.enter_context(nc.Block())
        LAST = NSUP - 1
        SC_M, SC_WO, SC_GCN = 0, 1, 2

        def typed(eng):
            eng.wait_ge(types_known, 1)
            return eng.If(eng.value_load(has_types[0:1, 0:1], min_val=0, max_val=1))

        @block.sync
        def _(sp):
            def load_x(s):
                sp.dma_start(x_all[:, s, :, :], x_rows[s, :, :, :]).then_inc(x_loaded, 16)

            def store_out(s):
                sp.wait_ge(o_added, KT * (s + 1))
                sp.dma_start(out_rows[s, :, :, :], x_all[:, s, :, :]).then_inc(stored, 16)

            sp.dma_start(w1_raw, W1[0:D, :].rearrange("(c p) e -> p c e", p=P)).then_inc(w1_loaded, 16)
            load_x(0)
            sp.dma_start(gcn_raw[:, :, 0:D], gcn_w.rearrange("(c p) e -> p c e", p=P)).then_inc(gcn_loaded, 16)
            sp.dma_start(gcn_raw[:, :, D:D + 1], gcn_b.rearrange("(c p o) -> p c o", p=P, o=1),
                         allow_slow_non_contiguous=True).then_inc(gcn_b_loaded, 16)
            sp.wait_ge(x_loaded, 16)
            sp.dma_start(adj_all[:, 0:HALF, :], adj_rows[:, 0:HALF, :]).then_inc(adj_loaded, 16)
            load_x(1)
            sp.dma_start(adj_all[:, HALF:, :], adj_rows[:, HALF:, :]).then_inc(adj_rest_loaded, 16)
            sp.dma_start(wo_raw[:, :, :], Wo.rearrange("(c p) e -> p c e", p=P)).then_inc(wo_loaded, 16)
            for s in range(2, 4):
                sp.wait_ge(x_loaded, 16 * s)
                load_x(s)

            with typed(sp):
                sp.dma_start(ty_emb[:, :], emb).then_inc(ty_emb_loaded, 16)
                with sp.Fori(0, NSUP) as s:
                    sp.wait_ge(ty_free, s + 1)
                    sp.dma_start(ty_x, x_rows[s, :, :, :]).then_inc(ty_loaded, 16)
                    sp.dma_start(ty_types, adj_rows[:, bass.ds(KT * s, KT), :]).then_inc(ty_loaded, 16)
                sp.wait_ge(ty_free, NSUP + 1)

            with sp.Fori(0, NSUP - 4) as s:
                sp.wait_ge(x_loaded, 16 * (s + 4))
                load_x(s + 4)
                store_out(s)
            with sp.Fori(NSUP - 4, LAST) as s:
                store_out(s)
            for k in range(KT):
                sp.wait_ge(o_added, KT * LAST + k + 1)
                sp.dma_start(out_rows[LAST, :, k, :], x_all[:, LAST, k, :]).then_inc(stored, 16)
            sp.wait_ge(stored, 16 * (LAST + KT))

        @block.gpsimd
        def _(pool):
            nc.gpsimd.memset(e_col[:, :], 1.0).then_inc(e_one, 1)
            nc.gpsimd.memset(ident[:, :], 0.0).then_inc(ident_zeroed, 1)
            nc.gpsimd.memset(ones[:, :], 1.0).then_inc(ones_made, 1)
            pool.wait_ge(ident_zeroed, 1)
            nc.gpsimd.affine_select(out=ident[:, :], in_=ident[:, :], compare_op=ALU.not_equal, fill=1.0,
                                    base=0, pattern=[[-1, P]], channel_multiplier=1).then_inc(ident_made, 1)
            nc.gpsimd.memset(attT_hi[:, :, :, :], 0.0).then_inc(attT_cleared, 1)

            def coefficients(s, stats, mul, add, counted):
                mean_e, mean_o, m2_e, m2_o = (stats[:, :, n] for n in (1, 4, 2, 5))
                done = 0

                def step(dst, in0, in1, op):
                    nonlocal done
                    if done:
                        pool.wait_ge(counted, COEF_STEPS * s + done)
                    nc.gpsimd.tensor_tensor(dst, in0, in1, op).then_inc(counted, 1)
                    done += 1

                step(root_sq, mean_e, mean_o, ALU.subtract)
                step(root_sq, root_sq, root_sq, ALU.mult)
                step(root_sq, root_sq, const["spread"], ALU.mult)
                step(var_d, m2_e, m2_o, ALU.add)
                step(var_d, var_d, root_sq, ALU.add)
                step(var_d, var_d, const["d_eps"], ALU.add)
                step(root, var_d, const["minus_half"], ALU.pow)
                step(var_d, var_d, const["minus_half"], ALU.mult)
                for _ in range(2):
                    step(root_sq, root, root, ALU.mult)
                    step(root_sq, root_sq, var_d, ALU.mult)
                    step(root_sq, root_sq, const["three_halves"], ALU.add)
                    step(root, root, root_sq, ALU.mult)
                step(mul, root, const["h_scale"], ALU.mult)
                step(root_sq, mean_e, mean_o, ALU.add)
                step(root_sq, root_sq, mul, ALU.mult)
                step(add, root_sq, const["minus_half"], ALU.mult)
                assert done == COEF_STEPS

            def main_coefficients(s):
                pool.wait_ge(stats_ready, s + 1)
                if not isinstance(s, int) or s >= 1:
                    pool.wait_ge(h_ready, KT * s)
                coefficients(s, stats6, ln_mul, ln_add, coef_ready)

            def g_low_parts(s):
                for c in range(DC):
                    pool.wait_ge(g_high, DC * s + c + 1)
                    nc.gpsimd.tensor_tensor(g_parts[:, c, :, 1, :], g_graphs[:, c, :, :], g_parts[:, c, :, 0, :],
                                            ALU.subtract).then_inc(g_split, 1)

            pool.dma_start(bo_all[:, 0, :], bo.partition_broadcast(P)).then_inc(bo_loaded, 16)
            for n, value in enumerate(const_values.values()):
                nc.gpsimd.memset(const_all[:, n, :], value)
            ins = nc.gpsimd.memset(minus_edge[:, :], -float(EDGE))
            ins.then_inc(consts_made, 1)
            pool.wait_ge(consts_made, 1)
            pool.wait_ge(ident_made, 1)
            nc.gpsimd.tensor_copy(ident16[:, :], ident[:, :]).then_inc(ident16_made, 1)
            main_coefficients(0)
            pool.wait_ge(weight_peaks, 1)
            nc.gpsimd.partition_all_reduce(peak_all[:, DC + 2:DC + 3], peak_part[:, DC + 2:DC + 3], P,
                                           ABSMAX).then_inc(weight_peaks_all, 1)
            pool.wait_ge(m_peaks, DC + 1)
            nc.gpsimd.partition_all_reduce(peak_all[:, 0:DC + 1], peak_part[:, 0:DC + 1], P,
                                           ABSMAX).then_inc(m_peaks_all, 1)
            main_coefficients(1)
            pool.wait_ge(top_types, QUARTERS)
            nc.gpsimd.partition_all_reduce(top_all[:, :], top_type[:, :], P, MAX).then_inc(top_types_all, 1)
            nc.gpsimd.tensor_scalar(bias_all[:, :, :], adj_all[:, :, :], -float(EDGE), HIDDEN,
                                    ALU.add, ALU.mult).then_inc(bias_made, 1)

            with typed(pool):
                with pool.Fori(0, NSUP) as s:
                    pool.wait_ge(ty_stats_ready, s + 1)
                    coefficients(s, ty_stats6, ty_ln_mul, ty_ln_add, ty_coef_ready)
                pool.wait_ge(ty_free, NSUP + 1)

            pool.wait_ge(wo_peak, 1)
            nc.gpsimd.partition_all_reduce(peak_all[:, DC + 1:DC + 2], peak_part[:, DC + 1:DC + 2], P,
                                           ABSMAX).then_inc(wo_peak_all, 1)
            pool.wait_ge(bo_loaded, 16)

            def iteration(s, prev=True, cur=True, nxt2=True):
                if cur and prev:
                    g_low_parts(s)
                if prev:
                    for c in (range(DC) if cur else (1,)):
                        pool.wait_ge(z_high, DC * (s - 1) + c + 1)
                        nc.gpsimd.tensor_tensor(z_lo[:, c, :], z32[:, c, :], z_hi[:, c, :],
                                                ALU.subtract).then_inc(z_split, 1)
                if nxt2:
                    main_coefficients(s + 2)
                if cur:
                    pool.wait_ge(h_ready, KT * (s + 1))
                    nc.gpsimd.tensor_tensor(x_all[:, s, :, :], x_all[:, s, :, :],
                                            bo_all[:, :, :].broadcast_to([P, KT, D]),
                                            ALU.add).then_inc(x_biased, 1)

            iteration(0, prev=False)
            iteration(1)
            with pool.Fori(2, LAST - 1) as s:
                iteration(s)
            iteration(LAST - 1, nxt2=False)
            iteration(LAST, nxt2=False)
            iteration(LAST + 1, cur=False, nxt2=False)

        @block.scalar
        def _(act):
            act.dma_start(w2_raw, W2[0:D, :].rearrange("(c p) e -> p c e", p=P)).then_inc(w2_loaded, 16)
            act.wait_ge(e_one, 1)
            act.dma_start(e_col[0:DE, :], emb[EDGE, :].rearrange("(k o) -> k o", o=1)).then_inc(e_loaded, 16)
            act.dma_start(w1_dep[0:DE, :], W1[D:D + DE, :]).then_inc(dep_loaded, 16)
            act.dma_start(w1_dep[DE:DE + 1, :], b1.rearrange("(o e) -> o e", o=1)).then_inc(dep_loaded, 16)
            act.dma_start(w2_dep[0:DE, :], W2[D:D + DE, :]).then_inc(dep_loaded, 16)
            act.dma_start(w2_dep[DE:DE + 1, :], b2.rearrange("(o e) -> o e", o=1)).then_inc(dep_loaded, 16)
            act.wait_ge(ones_made, 1)
            nc.scalar.activation(warm[:, :], ones[:, 0:1], ACT.Exp)

            def normalise(s):
                act.wait_ge(coef_ready, COEF_STEPS * (s + 1))
                if not isinstance(s, int) or s >= 1:
                    act.wait_ge(t_done, DC * s)
                for k in range(KT):
                    nc.scalar.activation(h_tok[:, k, :], x_all[:, s, k, :], ACT.Relu, bias=ln_add[:, k:k + 1],
                                         scale=ln_mul[:, k:k + 1]).then_inc(h_ready, 1)

            def transposed_high(s):
                if not isinstance(s, int) or s >= 1:
                    act.wait_ge(s_done, s)
                for c in range(DC):
                    act.wait_ge(t_done, DC * s + c + 1)
                    nc.scalar.activation(hT_hi[:, c, :], bank[T_BANK[c]][:, :], ACT.Copy).then_inc(t_high, 1)

            def g_chunk_out(s, c):
                act.wait_ge(g_done, DC * s + c + 1)
                nc.scalar.activation(g32[:, c, :], bank[G_BANK[c]][:, :], ACT.Identity,
                                     bias=pair_bias[:, c:c + 1], scale=PROJ).then_inc(g_copied, 1)

            def hg_high_part(s, k):
                act.wait_ge(hg_done, KT * s + k + 1)
                nc.scalar.activation(hg_hi[:, k, :], bank[HG_BANK[k]][:, 0:D], ACT.Copy,
                                     scale=PROJ).then_inc(hg_high, 1)

            def hg_move(s, k):
                act.wait_ge(hg_high, KT * s + k + 1)
                for g in range(GT):
                    nc.scalar.activation(hg_parts[S:2 * S, k, g, :], hg_hi[g * S:(g + 1) * S, k, :],
                                         ACT.Copy).then_inc(hg_moved, 1)

            def types_excess(n):
                if n == 0:
                    act.wait_ge(consts_made, 1)
                    act.wait_ge(adj_loaded, 16)
                if n == QUARTERS // 2:
                    act.wait_ge(adj_rest_loaded, 16)
                size = 2 * HALF // QUARTERS
                if n:
                    act.wait_ge(top_types, n)
                nc.scalar.activation(excess, adj_all[:, n * size:(n + 1) * size, :], ACT.Relu,
                                     bias=minus_edge[:, 0:1], accum_out=top_type[:, n:n + 1]).then_inc(top_types, 1)

            for c in range(DC):
                act.wait_ge(w_transposed, c + 1)
                nc.scalar.activation(w1T[:, c, :], bank[c][:, 0:D], ACT.Copy).then_inc(w_copied, 1)
            for c in range(DC):
                if c == DC - 1:
                    normalise(0)
                act.wait_ge(m_done, c + 1)
                nc.scalar.activation(m_raw[:, c, :], bank[c][:, 0:D], ACT.Copy).then_inc(m_copied, 1)
            act.wait_ge(weight_scales_ready, 1)
            for c in range(DC):
                nc.scalar.activation(gw_hi[:, c, 0:D], gcn_raw[:, c, 0:D], ACT.Copy,
                                     scale=scale[:, SC_GCN:SC_GCN + 1]).then_inc(gw_high, 1)
            transposed_high(0)
            types_excess(0)
            types_excess(1)
            hg_high_part(0, 0)
            act.wait_ge(m_scale_ready, 1)
            for c in range(DC):
                nc.scalar.activation(m_hi[:, c, :], m_raw[:, c, :], ACT.Copy,
                                     scale=scale[:, SC_M:SC_M + 1]).then_inc(m_high, 1)
            nc.scalar.activation(gw_hi[:, :, D], pair_vec[:, 1, :], ACT.Copy,
                                 scale=scale[:, SC_M:SC_M + 1]).then_inc(gw_high, 1)
            for k in range(1, KT):
                hg_high_part(0, k)
            types_excess(2)
            g_chunk_out(0, 0)
            types_excess(3)
            g_chunk_out(0, 1)
            g_chunk_out(0, 2)
            normalise(1)

            with typed(act):
                with act.Fori(0, NSUP) as s:
                    act.wait_ge(ty_coef_ready, COEF_STEPS * (s + 1))
                    for k in range(KT):
                        ins = nc.scalar.activation(ty_h[:, k, :], ty_x[:, k, :], ACT.Relu,
                                                   bias=ty_ln_add[:, k:k + 1], scale=ty_ln_mul[:, k:k + 1])
                    ins.then_inc(ty_h_ready, 1)
                act.wait_ge(ty_free, NSUP + 1)

            def iteration(s, prev=True, prev2=True, cur=True, nxt=True, nxt2=True):
                z_bank = Z_BANK if cur else LAST_Z_BANK
                for c in range(DC):
                    if cur and prev:
                        act.wait_ge(g_split, DC * (s - 1) + c + 1)
                        g_chunk_out(s, c)
                    if c == (0 if prev2 else DC - 1) and prev:
                        act.wait_ge(attT_done, s)
                        if prev2:
                            act.wait_ge(z_done, DC * (s - 1))
                        nc.scalar.activation(attT_parts[:, :, :, :], attT_bank[:, :, :, :],
                                             ACT.Copy).then_inc(attT_copied, 1)
                if prev and not prev2:
                    act.wait_ge(wo_scale_ready, 1)
                    nc.scalar.activation(wo_hi[:, :, :], wo_raw[:, :, :], ACT.Copy,
                                         scale=scale[:, SC_WO:SC_WO + 1]).then_inc(wo_high, 1)
                if prev:
                    for c in range(DC):
                        act.wait_ge(z_done, DC * (s - 1) + c + 1)
                        if prev2:
                            act.wait_ge(z_split, DC * (s - 2) + c + 1)
                        nc.scalar.activation(z32[:, c, :], bank[z_bank[c]][:, :], ACT.Relu,
                                             bias=gcn_bias[:, c:c + 1], scale=Z_DOWN).then_inc(z_copied, 1)
                if cur and prev:
                    act.wait_ge(z_done, DC * s)
                    if prev2:
                        for k in range(KT):
                            hg_high_part(s, k)
                            if k:
                                hg_move(s, k - 1)
                    else:
                        hg_high_part(s, 0)
                        hg_high_part(s, 1)
                        normalise(s + 1)
                        hg_high_part(s, 2)
                        hg_high_part(s, 3)
                if cur:
                    act.wait_ge(s_done, s + 1)
                    for part in range(2):
                        for g in range(GT):
                            nc.scalar.activation(score_parts[g * S:(g + 1) * S, part, :, :],
                                                 score_bank[part * S:(part + 1) * S, :, g, :],
                                                 ACT.Copy).then_inc(score_copied, 1)
                if nxt:
                    transposed_high(s + 1)
                if cur:
                    for k in range(KT - 1 if prev2 else 0, KT):
                        hg_move(s, k)
                    act.wait_ge(exp_bias_ready, s + 1)
                    for k in range(KT):
                        nc.scalar.activation(scores[:, k, :], scores[:, k, :], ACT.Exp,
                                             bias=exp_bias[:, k:k + 1], scale=exp_scale[:, 0:1],
                                             accum_out=row_sum[:, k:k + 1]).then_inc(exp_done, 1)
                if nxt2 and prev:
                    normalise(s + 2)

            iteration(0, prev=False, prev2=False)
            iteration(1, prev2=False)
            with act.Fori(2, LAST - 1) as s:
                iteration(s)
            iteration(LAST - 1, nxt2=False)
            iteration(LAST, nxt=False, nxt2=False)
            iteration(LAST + 1, cur=False, nxt=False, nxt2=False)

        @block.vector
        def _(dve):
            def statistics(s):
                dve.wait_ge(x_loaded, 16 * (s + 1))
                if not isinstance(s, int) or s >= 1:
                    dve.wait_ge(coef_ready, COEF_STEPS * s)
                for k in range(KT):
                    ins = nc.vector.bn_stats(stats6[:, k, :], x_all[:, s, k, :])
                ins.then_inc(stats_ready, 1)

            def transposed_low(s):
                for c in range(DC):
                    dve.wait_ge(t_high, DC * s + c + 1)
                    nc.vector.tensor_tensor(hT_lo[:, c, :], bank[T_BANK[c]][:, :], hT_hi[:, c, :],
                                            ALU.subtract).then_inc(t_split, 1)

            def magnitude(col, tensor, axis, counted):
                nc.vector.tensor_reduce(peak_part[:, col:col + 1], tensor, axis, ALU.max,
                                        apply_absolute_value=True).then_inc(counted, 1)

            def scales(lo, hi, base):
                dve.wait_ge(scale_step, base)
                nc.vector.tensor_scalar(peak_bits[:, lo:hi], peak[:, lo:hi].bitcast(i32), EXP_MASK, None,
                                        ALU.bitwise_and).then_inc(scale_step, 1)
                dve.wait_ge(scale_step, base + 1)
                nc.vector.tensor_scalar(flip_bits[:, lo:hi], peak_bits[:, lo:hi], -1.0, float(EXP_FLIP),
                                        ALU.mult, ALU.add).then_inc(scale_step, 1)
                nc.vector.tensor_scalar(unscale[:, lo:hi], peak_bits[:, lo:hi].bitcast(f32), 1.0 / W_TOP, None,
                                        ALU.mult).then_inc(scale_step, 1)
                dve.wait_ge(scale_step, base + 3)
                nc.vector.tensor_scalar(scale[:, lo:hi], flip_bits[:, lo:hi].bitcast(f32), W_TOP, None,
                                        ALU.mult).then_inc(scale_step, 1)
                dve.wait_ge(scale_step, base + 4)

            def low_part(low, raw, high, col):
                return nc.vector.scalar_tensor_tensor(low, raw, scale[:, col:col + 1], high,
                                                      ALU.mult, ALU.subtract)

            def hg_low_part(s, k):
                dve.wait_ge(hg_high, KT * s + k + 1)
                for g in range(GT):
                    rows = slice(g * S, (g + 1) * S)
                    nc.vector.scalar_tensor_tensor(hg_parts[0:S, k, g, :], bank[HG_BANK[k]][rows, 0:D], PROJ,
                                                   hg_hi[rows, k, :], ALU.mult, ALU.subtract)\
                      .then_inc(hg_split, 1)

            for c in range(DC):
                dve.wait_ge(w_transposed, DC + c + 1)
                nc.vector.tensor_copy(w2T[:, c, :], bank[3 + c][:, 0:D]).then_inc(w_copied, 1)
            statistics(0)
            dve.wait_ge(e_loaded, 16)
            nc.vector.tensor_copy(e_wide[:, :], e_col[:, :].broadcast_to([DE + 1, P])).then_inc(e_widened, 1)
            dve.wait_ge(gcn_loaded, 16)
            dve.wait_ge(gcn_b_loaded, 16)
            magnitude(DC + 2, gcn_raw[:, :, :], AX.XY, weight_peaks)

            def dot(out_col, rows, vector):
                if dots_made[0]:
                    dve.wait_ge(dot_done, dots_made[0])
                nc.vector.tensor_tensor_reduce(out=product[:, :], in0=rows, in1=vector, scale=1.0, scalar=0.0,
                                               op0=ALU.mult, op1=ALU.add, accum_out=out_col).then_inc(dot_done, 1)
                dots_made[0] += 1

            dots_made = [0]
            dve.wait_ge(pq_projected, 1)
            nc.vector.tensor_copy(q_row[:, :], bank[7][:, 0:D]).then_inc(q_copied, 1)
            for d in range(DC):
                dot(pair_vec[:, 0, d:d + 1], w2_raw[:, d, :], bank[6][:, 0:D])
            dve.wait_ge(m_copied, 1)
            magnitude(0, m_raw[:, 0, :], AX.X, m_peaks)
            dve.wait_ge(weight_peaks_all, 1)
            nc.vector.tensor_scalar(peak[:, SC_GCN:SC_GCN + 1], peak_all[:, DC + 2:DC + 3], TINY, None,
                                    ALU.max).then_inc(scale_step, 1)
            scales(SC_GCN, SC_GCN + 1, 1)
            nc.vector.tensor_scalar(gcn_bias[:, :], gcn_raw[:, :, D], scale[:, SC_GCN:SC_GCN + 1], Y_SCALE,
                                    ALU.mult, ALU.mult).then_inc(weight_scales_ready, 1)
            dve.wait_ge(q_copied, 1)
            for d in range(DC):
                dot(pair_vec[:, 1, d:d + 1], w1_raw[:, d, :], q_row[:, :])
            for c in range(1, DC):
                dve.wait_ge(m_copied, c + 1)
                magnitude(c, m_raw[:, c, :], AX.X, m_peaks)
            dve.wait_ge(dot_done, 2 * DC)
            magnitude(DC, pair_vec[:, :, :], AX.XY, m_peaks)
            for c in range(DC):
                dve.wait_ge(gw_high, c + 1)
                low_part(gw_lo[:, c, 0:D], gcn_raw[:, c, 0:D], gw_hi[:, c, 0:D], SC_GCN).then_inc(gw_split, 1)
            transposed_low(0)
            dve.wait_ge(m_peaks_all, 1)
            nc.vector.tensor_reduce(peak[:, SC_M:SC_M + 1], peak_all[:, 0:DC + 1], AX.X, ALU.max)\
              .then_inc(scale_step, 1)
            dve.wait_ge(scale_step, 6)
            nc.vector.tensor_scalar(peak[:, SC_M:SC_M + 1], peak[:, SC_M:SC_M + 1], TINY, None,
                                    ALU.max).then_inc(scale_step, 1)
            scales(SC_M, SC_M + 1, 7)
            nc.vector.tensor_scalar(pair_bias[:, :], pair_vec[:, 0, :], scale[:, SC_M:SC_M + 1], Y_SCALE,
                                    ALU.mult, ALU.mult).then_inc(m_scale_ready, 1)
            nc.vector.tensor_scalar(exp_scale[:, :], unscale[:, SC_M:SC_M + 1], 1.0 / S_SCALE, None, ALU.mult)
            nc.vector.tensor_scalar(exp_nscale[:, :], unscale[:, SC_M:SC_M + 1], -1.0 / S_SCALE, None, ALU.mult)
            statistics(1)
            hg_low_part(0, 0)
            for c in range(DC):
                dve.wait_ge(m_high, c + 1)
                low_part(m_lo[:, c, :], m_raw[:, c, :], m_hi[:, c, :], SC_M).then_inc(m_split, 1)
            dve.wait_ge(gw_high, DC + 1)
            low_part(gw_lo[:, :, D], pair_vec[:, 1, :], gw_hi[:, :, D], SC_M).then_inc(gw_vector, 1)

            def g_high_part(s, c):
                dve.wait_ge(g_copied, DC * s + c + 1)
                nc.vector.tensor_copy(g_parts[:, c, :, 0, :], g_graphs[:, c, :, :]).then_inc(g_high, 1)

            def first_g(c):
                g_high_part(0, c)
                dve.wait_ge(g_high, c + 1)
                nc.vector.tensor_tensor(g_parts[:, c, :, 1, :], g_graphs[:, c, :, :], g_parts[:, c, :, 0, :],
                                        ALU.subtract).then_inc(g_split, 1)

            hg_low_part(0, 1)
            hg_low_part(0, 2)
            hg_low_part(0, 3)
            dot(pq_all[:, :], q_row[:, :], bank[6][:, 0:D])
            dve.wait_ge(dot_done, 2 * DC + 1)
            nc.vector.tensor_scalar(pq_scaled[:, :], pq_all[:, :], scale[:, SC_M:SC_M + 1], S_SCALE,
                                    ALU.mult, ALU.mult).then_inc(scale_step, 1)
            first_g(0)
            dve.wait_ge(top_types_all, 1)
            nc.vector.tensor_reduce(top_one[:, :], top_all[:, :], AX.X, ALU.max).then_inc(top_types, 1)
            dve.wait_ge(top_types, QUARTERS + 1)
            nc.vector.tensor_scalar(has_types[:, :], top_one[:, :], 0.0, None,
                                    ALU.is_gt).then_inc(types_known, 1)
            first_g(1)
            first_g(2)
            dve.wait_ge(wo_loaded, 16)
            magnitude(DC + 1, wo_raw[:, :, :], AX.XY, wo_peak)

            with typed(dve):
                dve.wait_ge(ty_pe_setup, 1)
                nc.vector.memset(ty_embT[:, :], 1.0).then_inc(ty_dve_step, 1)
                dve.wait_ge(ty_dve_step, 1)
                nc.vector.tensor_copy(ty_embT[0:DE, :], bank[4][0:DE, 0:NT]).then_inc(ty_dve_setup, 1)
                dve.wait_ge(ty_pe_setup, 2)
                for n, vT in enumerate((ty_pT, ty_qT)):
                    at = n * DC * NT
                    nc.vector.tensor_copy(vT[:, :, :],
                                          bank[5][:, at:at + DC * NT].rearrange("p (c t) -> p c t", c=DC))\
                      .then_inc(ty_dve_step, 1)
                dve.wait_ge(ty_dve_step, 3)
                nc.vector.tensor_tensor(ty_pqT[:, :, :], ty_pT[:, :, :], ty_qT[:, :, :],
                                        ALU.mult).then_inc(ty_dve_setup, 1)
                dve.wait_ge(ty_pe_setup, 3)
                for n in range(2):
                    for c in range(DC):
                        at = (n * DC + c) * NT
                        nc.vector.tensor_scalar(ty_vec[:, n, c, :], bank[6][:, at:at + NT],
                                                pair_vec[:, n, c:c + 1], scale[:, SC_M:SC_M + 1],
                                                ALU.subtract, ALU.mult).then_inc(ty_dve_step, 1)
                nc.vector.tensor_scalar(ty_pq[:, :], bank[7][:, 0:NT], pq_all[:, 0:1], scale[:, SC_M:SC_M + 1],
                                        ALU.subtract, ALU.mult).then_inc(ty_dve_step, 1)
                for t in range(NT):
                    ins = nc.vector.memset(ty_value[:, t:t + 1], float(t))
                ins.then_inc(ty_dve_step, 1)
                dve.wait_ge(ty_dve_step, 2 * DC + 5)
                nc.vector.tensor_scalar(ty_vec[:, :, :, :], ty_vec[:, :, :, :], Y_SCALE, None,
                                        ALU.mult).then_inc(ty_dve_step, 1)
                nc.vector.tensor_scalar(ty_pq[:, :], ty_pq[:, :], S_SCALE, None, ALU.mult).then_inc(ty_dve_step, 1)
                dve.wait_ge(ty_dve_step, 2 * DC + 7)
                dve.wait_ge(bias_made, 1)
                nc.vector.sem_inc(ty_free, 1)
                with dve.Fori(0, NSUP) as s:
                    dve.wait_ge(ty_loaded, 32 * (s + 1))
                    here = bias_all[:, bass.ds(KT * s, KT), :]
                    nc.vector.tensor_scalar(here, ty_types, 1.0, -1.0, ALU.min, ALU.add).then_inc(ty_base_made, 1)
                    dve.wait_ge(ty_base_made, 2 * s + 1)
                    nc.vector.tensor_scalar(here, here, HIDDEN, None, ALU.mult).then_inc(ty_base_made, 1)
                    for k in range(KT):
                        ins = nc.vector.bn_stats(ty_stats6[:, k, :], ty_x[:, k, :])
                    ins.then_inc(ty_stats_ready, 1)
                    dve.wait_ge(ty_t_done, s + 1)
                    for c in range(DC):
                        ins = nc.vector.tensor_copy(ty_hT[:, c, :], bank[4 + c][:, :])
                    ins.then_inc(ty_hT_ready, 1)
                    dve.wait_ge(ty_rows_done, s + 1)
                    nc.vector.tensor_tensor(ty_row[:, :, :],
                                            bank[7][:, 0:KT * NT].rearrange("p (k t) -> p k t", k=KT),
                                            ty_pq[:, :].unsqueeze(1).broadcast_to([P, KT, NT]),
                                            ALU.add).then_inc(ty_rows_ready, 1)
                    with dve.Fori(TYPED.start, TYPED.stop) as t:
                        n = len(TYPED) * s + t - TYPED.start
                        nc.vector.tensor_copy(ty_stage, ty_vec[:, 0, :, bass.ds(t, 1)].broadcast_to([P, DC, P]))\
                          .then_inc(ty_staged, 1)
                        nc.vector.tensor_scalar(ty_equal, ty_types, ty_value[:, bass.ds(t, 1)], None,
                                                ALU.is_equal).then_inc(ty_equal_done, 1)
                        dve.wait_ge(ty_rows_ready, s + 1)
                        dve.wait_ge(ty_base_made, 2 * s + 2)
                        dve.wait_ge(ty_column_done, n + 1)
                        dve.wait_ge(ty_equal_done, n + 1)
                        for g in range(GT):
                            rows = slice(g * S, (g + 1) * S)
                            for k in range(KT):
                                at = k * P + g * S
                                nc.vector.scalar_tensor_tensor(
                                    ty_term[rows, k, :], bank[4][rows, at:at + S], ty_row[rows, k, bass.ds(t, 1)],
                                    ty_equal[rows, k, :], ALU.add, ALU.mult).then_inc(ty_term_done, 1)
                        dve.wait_ge(ty_term_done, GT * KT * (n + 1))
                        nc.vector.tensor_tensor(here, ty_term, here, ALU.add).then_inc(ty_added, 1)
                        dve.wait_ge(ty_added, n + 1)
                    nc.vector.sem_inc(ty_free, 1)

            def attention_high(s, prev2=True):
                dve.wait_ge(attT_copied, s)
                if prev2:
                    dve.wait_ge(z_done, DC * (s - 1))
                else:
                    dve.wait_ge(attT_cleared, 1)
                for g in range(GT):
                    nc.vector.tensor_copy(attT_hi[g * S:(g + 1) * S, :, g, :],
                                          attT_parts[0:S, :, g, :]).then_inc(attT_high, 1)

            def z_high_part(s, c):
                dve.wait_ge(z_copied, DC * s + c + 1)
                nc.vector.tensor_copy(z_hi[:, c, :], z32[:, c, :]).then_inc(z_high, 1)

            def add_output(s, tiles):
                dve.wait_ge(x_biased, s + 1)
                for k in tiles:
                    dve.wait_ge(o_done, KT * s + k + 1)
                    nc.vector.scalar_tensor_tensor(x_all[:, s, k, :], bank[O_BANK[k]][:, 0:D],
                                                   out_scale[:, 0:1], x_all[:, s, k, :],
                                                   ALU.mult, ALU.add).then_inc(o_added, 1)

            def iteration(s, prev=True, prev2=True, cur=True, nxt=True, nxt2=True):
                for c in range(DC):
                    if cur and prev:
                        if c == 0:
                            dve.wait_ge(s_done, s)
                        g_high_part(s, c)
                    if c == (0 if prev2 else DC - 1) and prev:
                        attention_high(s, prev2)
                if prev and not prev2:
                    dve.wait_ge(wo_high, 1)
                    low_part(wo_lo[:, :, :], wo_raw[:, :, :], wo_hi[:, :, :], SC_WO).then_inc(wo_split, 1)
                if prev:
                    for c in range(DC):
                        if prev2 and c == 0:
                            dve.wait_ge(o_done, KT * (s - 1))
                        z_high_part(s - 1, c)
                if nxt2 and (prev2 or not prev):
                    statistics(s + 2)
                if cur:
                    if prev:
                        for k in range(KT):
                            dve.wait_ge(hg_high, KT * s + k + 1)
                            nc.vector.tensor_scalar(row_term[:, k:k + 1], bank[HG_BANK[k]][:, D:D + 1], Y_SCALE,
                                                    pq_scaled[:, 0:1], ALU.mult, ALU.add).then_inc(row_ready, 1)
                            hg_low_part(s, k)
                    else:
                        dve.wait_ge(first_rows_done, 1)
                        dve.wait_ge(scale_step, 12)
                        nc.vector.tensor_scalar(row_term[:, :], bank[7][:, 0:KT], Y_SCALE, pq_scaled[:, 0:1],
                                                ALU.mult, ALU.add).then_inc(row_ready, KT)
                    if prev and not prev2:
                        statistics(s + 2)
                    if not prev:
                        transposed_low(1)
                    if not prev:
                        dve.wait_ge(bias_made, 1)
                    dve.wait_ge(row_ready, KT * (s + 1))
                    for k in range(KT):
                        nc.vector.tensor_scalar(masks[:, k, :], bias_all[:, KT * s + k, :], row_term[:, k:k + 1],
                                                None, ALU.add).then_inc(masked, 1)
                    dve.wait_ge(score_copied, 2 * GT * (s + 1))
                    nc.vector.tensor_tensor(scores[:, :, :], score_parts[:, 0, :, :], score_parts[:, 1, :, :],
                                            ALU.add).then_inc(summed, 1)
                    dve.wait_ge(summed, s + 1)
                    dve.wait_ge(masked, KT * (s + 1))
                    nc.vector.tensor_tensor(scores[:, :, :], scores[:, :, :], masks[:, :, :],
                                            ALU.add).then_inc(scored, 1)
                    dve.wait_ge(scored, s + 1)
                    nc.vector.tensor_reduce(row_max[:, :], scores[:, :, :], AX.X, ALU.max).then_inc(maxed, 1)
                    dve.wait_ge(maxed, s + 1)
                    nc.vector.tensor_scalar(exp_bias[:, :], row_max[:, :], exp_nscale[:, 0:1], None,
                                            ALU.mult).then_inc(exp_bias_ready, 1)
                if nxt and prev:
                    transposed_low(s + 1)
                early = 1 if nxt else 2
                if prev:
                    add_output(s - 1, range(early))
                if not prev:
                    dve.wait_ge(wo_peak_all, 1)
                    nc.vector.tensor_scalar(peak[:, SC_WO:SC_WO + 1], peak_all[:, DC + 1:DC + 2], TINY, None,
                                            ALU.max).then_inc(scale_step, 1)
                    scales(SC_WO, SC_WO + 1, 13)
                    nc.vector.tensor_scalar(out_half[:, :], unscale[:, SC_GCN:SC_GCN + 1], 1.0 / Y_SCALE, None,
                                            ALU.mult).then_inc(wo_scale_ready, 1)
                    dve.wait_ge(wo_scale_ready, 1)
                    nc.vector.tensor_scalar(out_scale[:, :], out_half[:, :], unscale[:, SC_WO:SC_WO + 1], None,
                                            ALU.mult).then_inc(scale_step, 1)
                if cur:
                    dve.wait_ge(exp_done, KT * (s + 1))
                    nc.vector.reciprocal(row_inv[:, :], row_sum[:, :]).then_inc(inverted, 1)
                    dve.wait_ge(inverted, s + 1)
                    nc.vector.tensor_tensor(att[:, :, :], scores[:, :, :],
                                            row_inv[:, :].unsqueeze(2).broadcast_to([P, KT, S]),
                                            ALU.mult).then_inc(weighted, 1)
                    dve.wait_ge(weighted, s + 1)
                    if prev:
                        dve.wait_ge(attT_done, s)
                    nc.vector.tensor_scalar(att_parts[:, :, 0, :], att[:, :, :], A_SCALE, None,
                                            ALU.mult).then_inc(att_high, 1)
                    dve.wait_ge(att_high, s + 1)
                    nc.vector.scalar_tensor_tensor(att_parts[:, :, 1, :], att[:, :, :], A_SCALE,
                                                   att_parts[:, :, 0, :], ALU.mult, ALU.subtract)\
                      .then_inc(att_ready, 1)
                if prev and nxt:
                    add_output(s - 1, range(early, KT))

            def last_aggregation():
                attention_high(LAST + 1)
                add_output(LAST - 1, range(2, KT))
                dve.wait_ge(o_done, KT * LAST)
                for c in (0, 1):
                    z_high_part(LAST, c)
                z_low_part(0)
                z_high_part(LAST, 2)
                z_low_part(2)

            def z_low_part(c):
                dve.wait_ge(z_high, DC * LAST + c + 1)
                nc.vector.tensor_tensor(z_lo[:, c, :], z32[:, c, :], z_hi[:, c, :],
                                        ALU.subtract).then_inc(last_z_split, 1)

            iteration(0, prev=False, prev2=False)
            iteration(1, prev2=False)
            with dve.Fori(2, LAST - 1) as s:
                iteration(s)
            iteration(LAST - 1, nxt2=False)
            iteration(LAST, nxt=False, nxt2=False)
            last_aggregation()
            add_output(LAST, range(KT))

        @block.tensor
        def _(pe):
            def split_product(dst, left, right, before=None):
                last = None
                for c in range(DC):
                    if before:
                        before(c)
                    (lh, ll), (rh, rl) = left(c), right(c)
                    nc.tensor.matmul(dst, lh, rh, start=(c == 0), stop=False)
                    nc.tensor.matmul(dst, lh, rl, start=False, stop=False)
                    last = nc.tensor.matmul(dst, ll, rh, start=False, stop=(c == DC - 1))
                return last

            def hg_read(tiles):
                pe.wait_ge(hg_split, GT * tiles)

            pe.wait_ge(ident_made, 1)
            for n, raw, loaded in ((0, w1_raw, w1_loaded), (DC, w2_raw, w2_loaded)):
                pe.wait_ge(loaded, 16)
                for c in range(DC):
                    for d in range(DC):
                        last = nc.tensor.transpose(bank[n + c][:, d * P:(d + 1) * P],
                                                   raw[:, d, c * P:(c + 1) * P], ident[:, :])
                    last.then_inc(w_transposed, 1)
            pe.wait_ge(w_copied, 2 * DC)
            for d in range(DC):
                for c in range(DC):
                    last = nc.tensor.matmul(bank[d][:, 0:D], w1T[:, c, d * P:(d + 1) * P], w2T[:, c, :],
                                            start=(c == 0), stop=(c == DC - 1))
                last.then_inc(m_done, 1)
                if d == 0:
                    pe.wait_ge(dep_loaded, 16 * 4)
                    pe.wait_ge(e_widened, 1)
                    nc.tensor.matmul(bank[6][:, 0:D], e_wide[:, :], w1_dep[:, :], start=True, stop=True)
                    nc.tensor.matmul(bank[7][:, 0:D], e_wide[:, :], w2_dep[:, :], start=True, stop=True)\
                      .then_inc(pq_projected, 1)

            def transposes(s, prev=True, after_g=False):
                pe.wait_ge(h_ready, KT * (s + 1))
                for c in range(DC):
                    if prev and c < 2:
                        pe.wait_ge(z_copied, DC * (s - 2) + c + 2)
                    if c == 2 and prev:
                        hg_read(KT * (s - 1) + 3)
                    if c == 2 and after_g:
                        pe.wait_ge(g_copied, DC)
                    for k in range(KT):
                        last = nc.tensor.transpose(bank[T_BANK[c]][:, k * P:(k + 1) * P],
                                                   h_tok[:, k, c * P:(c + 1) * P], ident[:, :])
                    last.then_inc(t_done, 1)

            def scores_of(s):
                for k in range(KT):
                    for g in range(GT):
                        cols = slice(k * P + g * S, k * P + (g + 1) * S)
                        for d in range(DC):
                            for n, part in enumerate((hT_hi, hT_lo)):
                                last = nc.tensor.matmul(score_bank[:, k, g, :], g_parts[:, d, GT * k + g, :, :],
                                                        part[:, d, cols], start=(d == 0 and n == 0),
                                                        stop=(d == DC - 1 and n == 1))
                last.then_inc(s_done, 1)

            def g_chunk(c, before=None):
                split_product(bank[G_BANK[c]][:, :],
                              lambda d: (m_hi[:, d, c * P:(c + 1) * P], m_lo[:, d, c * P:(c + 1) * P]),
                              lambda d: (hT_hi[:, d, :], hT_lo[:, d, :]), before).then_inc(g_done, 1)

            pe.wait_ge(m_copied, DC)
            transposes(0, prev=False)

            def chunk_ready(s):
                def wait(d):
                    if isinstance(s, int) and s == 0:
                        pe.wait_ge(gw_split, d + 1)
                    pe.wait_ge(t_split, DC * s + d + 1)
                return wait

            for k in range(KT):
                rows = slice(k * P, (k + 1) * P)
                split_product(bank[HG_BANK[k]][:, 0:D],
                              lambda d: (hT_hi[:, d, rows], hT_lo[:, d, rows]),
                              lambda d: (gw_hi[:, d, 0:D], gw_lo[:, d, 0:D]),
                              chunk_ready(0) if k == 0 else None).then_inc(hg_done, 1)

            for c in range(DC):
                hg_read(c + 1)
                g_chunk(c, (lambda d: pe.wait_ge(m_split, d + 1)) if c == 0 else None)
            with typed(pe):
                pe.wait_ge(ty_emb_loaded, 16)
                nc.tensor.transpose(bank[4][0:DE, 0:NT], ty_emb[:, :], ident[0:NT, 0:NT]).then_inc(ty_pe_setup, 1)
                pe.wait_ge(ty_dve_setup, 1)
                for n, dep in ((0, w1_dep), (DC, w2_dep)):
                    for c in range(DC):
                        last = nc.tensor.matmul(bank[5][:, (n + c) * NT:(n + c + 1) * NT],
                                                dep[:, c * P:(c + 1) * P], ty_embT[:, :], start=True, stop=True)
                last.then_inc(ty_pe_setup, 1)
                pe.wait_ge(ty_dve_setup, 2)
                for n, (wT, vT) in enumerate(((w2T, ty_pT), (w1T, ty_qT))):
                    for d in range(DC):
                        at = (n * DC + d) * NT
                        for c in range(DC):
                            nc.tensor.matmul(bank[6][:, at:at + NT], wT[:, c, d * P:(d + 1) * P], vT[:, c, :],
                                             start=(c == 0), stop=(c == DC - 1))
                for c in range(DC):
                    last = nc.tensor.matmul(bank[7][:, 0:NT], ones[:, :], ty_pqT[:, c, :],
                                            start=(c == 0), stop=(c == DC - 1))
                last.then_inc(ty_pe_setup, 1)
                pe.wait_ge(ty_free, 1)
                with pe.Fori(0, NSUP) as s:
                    pe.wait_ge(ty_h_ready, s + 1)
                    for c in range(DC):
                        for k in range(KT):
                            last = nc.tensor.transpose(bank[4 + c][:, k * P:(k + 1) * P],
                                                       ty_h[:, k, c * P:(c + 1) * P], ident[:, :])
                    last.then_inc(ty_t_done, 1)
                    pe.wait_ge(ty_hT_ready, s + 1)
                    for k in range(KT):
                        for c in range(DC):
                            last = nc.tensor.matmul(bank[7][:, k * NT:(k + 1) * NT], ty_hT[:, c, k * P:(k + 1) * P],
                                                    ty_vec[:, 1, c, :], start=(c == 0), stop=(c == DC - 1))
                    last.then_inc(ty_rows_done, 1)
                    with pe.Fori(TYPED.start, TYPED.stop) as t:
                        pe.wait_ge(ty_staged, len(TYPED) * s + t - TYPED.start + 1)
                        for c in range(DC):
                            last = nc.tensor.matmul(bank[4][:, :], ty_stage[:, c, :], ty_hT[:, c, :],
                                                    start=(c == 0), stop=(c == DC - 1))
                        last.then_inc(ty_column_done, 1)
                pe.wait_ge(ty_free, NSUP + 1)

            pe.wait_ge(gw_vector, 1)
            for k in range(KT):
                rows = slice(k * P, (k + 1) * P)
                last = split_product(bank[7][:, k:k + 1],
                                     lambda d: (hT_hi[:, d, rows], hT_lo[:, d, rows]),
                                     lambda d: (gw_hi[:, d, D:D + 1], gw_lo[:, d, D:D + 1]))
            last.then_inc(first_rows_done, 1)
            pe.wait_ge(g_split, DC)
            pe.wait_ge(dot_done, 2 * DC + 1)
            scores_of(0)
            transposes(1, prev=False, after_g=True)

            def iteration(s, prev2=True, cur=True, nxt=True):
                def transposed_attention():
                    pe.wait_ge(att_ready, s)
                    if prev2:
                        pe.wait_ge(attT_high, GT * (s - 1))
                        pe.wait_ge(attT_copied, s - 1)
                    else:
                        pe.wait_ge(ident16_made, 1)
                    for k in range(KT):
                        last = nc.tensor.transpose(attT_bank[:, k, :, :], att_parts[:, k, :, :], ident16[:, :])
                    last.then_inc(attT_done, 1)

                def hg_tile(k):
                    rows = slice(k * P, (k + 1) * P)
                    if k < DC:
                        pe.wait_ge(g_copied, DC * s + k + 1)
                    else:
                        pe.wait_ge(z_copied, DC * (s - 1) + 1)
                    split_product(bank[HG_BANK[k]][:, 0:D + 1],
                                  lambda d: (hT_hi[:, d, rows], hT_lo[:, d, rows]),
                                  lambda d: (gw_hi[:, d, :], gw_lo[:, d, :])).then_inc(hg_done, 1)

                early = 0 if prev2 else 2
                for c in range(DC):
                    if cur:
                        if c < 2 and prev2:
                            pe.wait_ge(o_added, KT * (s - 2) + c + 1)
                        g_chunk(c, chunk_ready(s) if c == 0 else None)
                    if c == 0 and prev2:
                        transposed_attention()
                if not prev2:
                    hg_tile(0)
                    transposed_attention()
                    hg_tile(1)
                pe.wait_ge(attT_high, GT * s)
                pe.wait_ge(attT_copied, s)
                hg_read(KT * s)
                pe.wait_ge(hg_moved, GT * KT * s)
                z_bank = Z_BANK if cur else LAST_Z_BANK
                for c in range(DC):
                    if prev2 and cur and c < 2:
                        pe.wait_ge(o_added, KT * (s - 2) + c + 3)
                    if not cur and c == 2:
                        pe.wait_ge(score_copied, 2 * GT * NSUP)
                    for k in range(KT):
                        cols = slice(c * P, (c + 1) * P)
                        nc.tensor.matmul(bank[z_bank[c]][:, k * P:(k + 1) * P], hg_hi[:, k, cols],
                                         attT_hi[:, k, :, :], start=True, stop=False)
                        for g in range(GT):
                            at = k * P + g * S
                            last = nc.tensor.matmul(bank[z_bank[c]][:, at:at + S], hg_parts[:, k, g, cols],
                                                    attT_parts[:, k, g, :], start=False, stop=(g == GT - 1))
                    last.then_inc(z_done, 1)
                if cur:
                    for k in range(early, KT):
                        hg_tile(k)
                    pe.wait_ge(g_split, DC * (s + 1))
                    pe.wait_ge(score_copied, 2 * GT * s)
                    scores_of(s)
                if nxt:
                    transposes(s + 1)
                if not cur:
                    return
                if not prev2:
                    pe.wait_ge(wo_split, 1)
                pe.wait_ge(z_split, DC * s)
                for k in range(KT):
                    rows = slice(k * P, (k + 1) * P)
                    if k < DC:
                        hg_read(KT * s + (1, 2, 4)[k])
                    elif nxt:
                        pe.wait_ge(t_split, DC * (s + 1) + 1)
                    split_product(bank[O_BANK[k]][:, 0:D],
                                  lambda e: (z_hi[:, e, rows], z_lo[:, e, rows]),
                                  lambda e: (wo_hi[:, e, :], wo_lo[:, e, :])).then_inc(o_done, 1)

            def last_output():
                for e in range(DC):
                    pe.wait_ge(z_high, DC * LAST + e + 1)
                    for k in range(KT):
                        if e == 0:
                            pe.wait_ge(o_added, KT * (LAST - 1) + k + 1)
                        z_rows = z_hi[:, e, k * P:(k + 1) * P]
                        nc.tensor.matmul(bank[O_BANK[k]][:, 0:D], z_rows, wo_hi[:, e, :],
                                         start=(e == 0), stop=False)
                        nc.tensor.matmul(bank[O_BANK[k]][:, 0:D], z_rows, wo_lo[:, e, :], start=False, stop=False)
                pe.wait_ge(z_split, DC * LAST + 1)
                pe.wait_ge(last_z_split, DC - 1)
                for k in range(KT):
                    for e in range(DC):
                        last = nc.tensor.matmul(bank[O_BANK[k]][:, 0:D], z_lo[:, e, k * P:(k + 1) * P],
                                                wo_hi[:, e, :], start=False, stop=(e == DC - 1))
                    last.then_inc(o_done, 1)

            iteration(1, prev2=False)
            with pe.Fori(2, LAST) as s:
                iteration(s)
            iteration(LAST, nxt=False)
            iteration(LAST + 1, cur=False, nxt=False)
            last_output()


_INS = ['x', 'adj', 'L0_gnn_dep_emb_table', 'L0_gnn_W1_w', 'L0_gnn_W1_b', 'L0_gnn_W2_w', 'L0_gnn_W2_b',
        'L0_gnn_gcn_w', 'L0_gnn_gcn_b', 'L0_gnn_Wo_w', 'L0_gnn_Wo_b']


def kernel(**inputs):
    import numpy as _np
    import concourse.bacc as _bacc
    from concourse import mybir as _mybir
    from concourse.bass_utils import run_bass_kernel_spmd as _run

    nc = _bacc.Bacc("TRN2", target_bir_lowering=False, num_devices=1)
    arrays, args = {}, []
    for name in _INS:
        a = _np.ascontiguousarray(inputs[name])
        arrays[f"in_{name}_dram"] = a
        args.append(nc.dram_tensor(f"in_{name}_dram", a.shape, _mybir.dt.from_np(a.dtype), kind="ExternalInput").ap())
    shape = inputs['x'].shape
    args.append(nc.dram_tensor("out_0_dram", shape, _mybir.dt.float32, kind="ExternalOutput").ap())
    gnn_layer_program(nc, *args)
    r = _run(nc, [arrays], core_ids=[0])
    return r.results[0]["out_0_dram"]
```
